# Optimizing a Trainium2 kernel written in Bass

```python
import numpy as np
import jax
import jax.numpy as jnp

def _softmax(x, axis=-1):
    return jax.nn.softmax(x, axis=axis)

def _gelu(x):
    return jax.nn.gelu(x, approximate=True)

def _silu(x):
    return jax.nn.silu(x)

def _sigmoid(x):
    return jax.nn.sigmoid(x)

def _layernorm(x, axis=-1, eps=1e-05):
    m = jnp.mean(x, axis=axis, keepdims=True)
    v = jnp.var(x, axis=axis, keepdims=True)
    return (x - m) / jnp.sqrt(v + eps)

def _scatter_add(tgt, idx, src, axis=0):
    return tgt.at[idx].add(src)

def _segment_sum(src, seg, n):
    return jax.ops.segment_sum(src, seg, n)
kernel_name = 'mk_gnn_resnorm_d1_gnn_r8_a45830'

def setup_inputs(seed: int=0):
    np.random.seed(seed)
    _w = jnp.asarray

    def _rec_inputs():
        import jax
        import jax.numpy as jnp
        _gk = jax.random.key(seed)
        x = -0.000202 + 1 * jax.random.normal(jax.random.fold_in(_gk, 1), (6250, 128), jnp.float32)
        src = jax.random.randint(jax.random.fold_in(_gk, 2), (200000,), 0, 6250, jnp.int32)
        dst = jax.random.randint(jax.random.fold_in(_gk, 3), (200000,), 0, 6250, jnp.int32)
        _o = jnp.argsort(dst, stable=True)
        src = src[_o]
        dst = dst[_o]
        edge_type_3 = jax.random.randint(jax.random.fold_in(_gk, 12), (200000,), 0, 3, jnp.int32)
        return (x, src, dst, edge_type_3)
    x, src, dst, edge_type_3 = _rec_inputs()

    def _L0_gnn_setup():
        import jax, jax.numpy as jnp
        import numpy as np
        N_NODES = 6250
        N_EDGES = 37500
        INPUT_DIM = 128
        HIDDEN_DIM = 256
        NUM_HEADS = 8
        HEAD_DIM = HIDDEN_DIM // NUM_HEADS
        NUM_EDGE_TYPES = 3
        key = jax.random.key(seed)
        ks = jax.random.split(key, 12)
        s_in = 1.0 / np.sqrt(INPUT_DIM)
        s_hid = 1.0 / np.sqrt(HIDDEN_DIM)
        return {'node_features': jax.random.normal(ks[0], (N_NODES, INPUT_DIM), jnp.float32), 'edges': jax.random.randint(ks[1], (N_EDGES, 2), 0, N_NODES), 'edge_types': jax.random.randint(ks[2], (N_EDGES,), 0, NUM_EDGE_TYPES), 'Wq': jax.random.normal(ks[3], (HIDDEN_DIM, INPUT_DIM), jnp.float32) * s_in, 'bq': jax.random.normal(ks[4], (HIDDEN_DIM,), jnp.float32) * s_in, 'Wk': jax.random.normal(ks[5], (HIDDEN_DIM, INPUT_DIM), jnp.float32) * s_in, 'bk': jax.random.normal(ks[6], (HIDDEN_DIM,), jnp.float32) * s_in, 'Wv': jax.random.normal(ks[7], (HIDDEN_DIM, INPUT_DIM), jnp.float32) * s_in, 'bv': jax.random.normal(ks[8], (HIDDEN_DIM,), jnp.float32) * s_in, 'edge_emb': jax.random.normal(ks[9], (NUM_EDGE_TYPES, HIDDEN_DIM), jnp.float32), 'Wo': jax.random.normal(ks[10], (INPUT_DIM, HIDDEN_DIM), jnp.float32) * s_hid, 'bo': jax.random.normal(ks[11], (INPUT_DIM,), jnp.float32) * s_hid}
    _L0_gnn_all = _L0_gnn_setup()
    _L0_gnn_in = {k: v for k, v in _L0_gnn_all.items() if k in ('Wq', 'bq', 'Wk', 'bk', 'Wv', 'bv', 'edge_emb', 'Wo', 'bo')}
    del _L0_gnn_all
    return {'x': x, 'src': src, 'dst': dst, 'edge_type_3': edge_type_3, 'L0_gnn_Wq': _L0_gnn_in['Wq'], 'L0_gnn_bq': _L0_gnn_in['bq'], 'L0_gnn_Wk': _L0_gnn_in['Wk'], 'L0_gnn_bk': _L0_gnn_in['bk'], 'L0_gnn_Wv': _L0_gnn_in['Wv'], 'L0_gnn_bv': _L0_gnn_in['bv'], 'L0_gnn_edge_emb': _L0_gnn_in['edge_emb'], 'L0_gnn_Wo': _L0_gnn_in['Wo'], 'L0_gnn_bo': _L0_gnn_in['bo']}

def reference(x, src, dst, edge_type_3, L0_gnn_Wq, L0_gnn_bq, L0_gnn_Wk, L0_gnn_bk, L0_gnn_Wv, L0_gnn_bv, L0_gnn_edge_emb, L0_gnn_Wo, L0_gnn_bo):
    import jax
    import jax.numpy as jnp

    def _L0_gnn_ref(node_features, edges, edge_types, Wq, bq, Wk, bk, Wv, bv, edge_emb, Wo, bo):
        import jax, jax.numpy as jnp
        import numpy as np
        N_NODES = 6250
        N_EDGES = 37500
        INPUT_DIM = 128
        HIDDEN_DIM = 256
        NUM_HEADS = 8
        HEAD_DIM = HIDDEN_DIM // NUM_HEADS
        NUM_EDGE_TYPES = 3
        Q = (node_features @ Wq.T + bq).reshape(-1, NUM_HEADS, HEAD_DIM)
        K = (node_features @ Wk.T + bk).reshape(-1, NUM_HEADS, HEAD_DIM)
        V = (node_features @ Wv.T + bv).reshape(-1, NUM_HEADS, HEAD_DIM)
        src = edges[:, 0]
        tgt = edges[:, 1]
        scale = 1.0 / jnp.sqrt(jnp.float32(HEAD_DIM))
        scores = jnp.einsum('ehd,egd->ehg', Q[src], K[tgt]) * scale
        attn = jax.nn.softmax(scores, axis=-1)
        msg = jnp.einsum('ehg,egd->ehd', attn, V[tgt]).reshape(-1, HIDDEN_DIM)
        msg = msg + edge_emb[edge_types]
        out_e = msg @ Wo.T + bo
        messages = jax.ops.segment_sum(out_e, src, num_segments=N_NODES)
        return messages
    edge_index_t = jnp.stack([src, dst], axis=1)
    x = _layernorm(x + _L0_gnn_ref(x, edge_index_t, edge_type_3, L0_gnn_Wq, L0_gnn_bq, L0_gnn_Wk, L0_gnn_bk, L0_gnn_Wv, L0_gnn_bv, L0_gnn_edge_emb, L0_gnn_Wo, L0_gnn_bo), axis=-1)
    return x

_drawn_inputs = setup_inputs


def setup_inputs(seed=0):
    import zlib

    import numpy as np

    out = dict(_drawn_inputs(seed))
    spreads = {}
    factors = {'L0_gnn_bq': 5.462, 'L0_gnn_bk': 5.102}
    for name, (base, spread) in spreads.items():
        noise = np.random.default_rng([zlib.crc32(name.encode()), seed]).standard_normal(out[name].shape)
        drawn = base * np.exp(spread * noise) if base else spread * noise
        out[name] = jnp.asarray(drawn.astype(out[name].dtype))
    for name, factor in factors.items():
        out[name] = (out[name] * factor).astype(out[name].dtype)
    return out
```

```python
import numpy as np
import concourse.bass as bass
from concourse import mybir
from contextlib import ExitStack

FP32 = mybir.dt.float32
BF16 = mybir.dt.bfloat16
I32 = mybir.dt.int32
U32 = mybir.dt.uint32
ALU = mybir.AluOpType
ACT = mybir.ActivationFunctionType
AX = mybir.AxisListType

P = 128
N = 6250
E = 200000
D = 128
HD = 256
H = 8
DH = HD // H
KINDS = 3
NT = -(-N // P)
TAIL = N - (NT - 1) * P
EPS = 1e-5
SCALE = 1.0 / float(np.sqrt(np.float32(DH)))

GT = 8
GROUPS = 2 * (-(-E // (2 * GT * P)))
ET = GROUPS * GT
EFULL = E // P
HI = NT + 1
PADKEY = NT * P + P - 1
KCOLS = KINDS * NT

SLOTS = 8
BLOCKS = (E + (SLOTS - 1) * N) // SLOTS
NS = -(-BLOCKS // P)
TPS = SLOTS
SUP = P * SLOTS
BT = 4
BPT = 4
TROWS = N + P


def build(nc, x, src, dst, kind, wq, bq, wk, bk, wv, bv, emb, wo, bo, out):
    with ExitStack() as ctx:
        def sb(name, shape, dt=FP32, c=ctx):
            return c.enter_context(nc.sbuf_tensor(name, shape, dt))

        def sem(name):
            return ctx.enter_context(nc.semaphore(name))

        q_tab = nc.dram_tensor("q_tab", [NT * P, HD], FP32).ap()
        kv_tab = nc.dram_tensor("kv_tab", [NT * P, 2 * HD], FP32).ap()
        key_rows = nc.dram_tensor("key_rows", [ET, P], I32).ap()
        rec = nc.dram_tensor("rec", [NS * SUP, 2], I32).ap()
        sums = nc.dram_tensor("sums", [TROWS, D], FP32).ap()

        ident = sb("ident", [P, P])
        below = sb("below", [P, P])
        above = sb("above", [P, P])
        iota_row_i = sb("iota_row_i", [P, KCOLS], I32)
        iota_row = sb("iota_row", [P, KCOLS], BF16)
        part_i = sb("part_i", [P, 1], I32)
        part_f = sb("part_f", [P, 1])
        blk_i = sb("blk_i", [P, 1], I32)
        blk_f = sb("blk_f", [P, 1])
        own = sb("own", [P, BPT])
        trash = sb("trash", [P, 1])
        wo4 = sb("wo4", [P, H, D])
        kindw = sb("kindw", [P, KINDS, D])
        key_c = sb("key_c", [P, ET])
        dst_c = sb("dst_c", [P, ET])
        lo_c = sb("lo_c", [P, ET])
        hi_c = sb("hi_c", [P, ET])
        cid_c = sb("cid_c", [P, ET])
        counts = sb("counts", [P, KINDS, NT])
        first_slot = sb("first_slot", [P, HI])
        kv = sb("kv", [P, 4, BT, 2 * HD])

        DCH = sem("DCH")
        pass_sp, pass_pool, pass_pe = sem("pass_sp"), sem("pass_pool"), sem("pass_pe")

        with ExitStack() as c0:
            wl = sb("wl", [P, 6, D], FP32, c0)
            wt = sb("wt", [P, 6 * P], FP32, c0)
            bias = sb("bias", [P, 3, HD], FP32, c0)
            wol = sb("wol", [P, HD], FP32, c0)
            wot = sb("wot", [P, 2, D], FP32, c0)
            bob = sb("bob", [P, D], FP32, c0)
            embt = sb("embt", [P, KINDS, 2], FP32, c0)
            xin = sb("xin", [P, 2, D], FP32, c0)
            xt = sb("xt", [P, 2, P], FP32, c0)
            qkv = sb("qkv", [P, 2, 3 * HD], FP32, c0)
            zero = sb("zero", [P, D], FP32, c0)
            fill = kv[:, :, :, :].rearrange("p a b c -> p (a b c)").bitcast(I32)
            pw = c0.enter_context(nc.psum_tensor("pw", [P, 1024], FP32))
            px = c0.enter_context(nc.psum_tensor("px", [P, 2, 512], FP32))
            pq = c0.enter_context(nc.psum_tensor("pq", [P, 2, 2, 512], FP32))
            HALF = 3 * HD // 2

            weights_in, emb_in, bias_in = sem("weights_in"), sem("emb_in"), sem("bias_in")
            consts, wt_done, wo_done, wo_copied = sem("consts"), sem("wt_done"), sem("wo_done"), sem("wo_copied")
            wt_copied, kindw_done, pads_set = sem("wt_copied"), sem("kindw_done"), sem("pads_set")
            x_in = [sem("x_in0"), sem("x_in1")]
            x_turned, xt_copied, qkv_done, qkv_biased = sem("x_turned"), sem("xt_copied"), sem("qkv_done"), sem("qkv_biased")
            qkv_out = [sem("qkv_out0"), sem("qkv_out1")]
            inits_out, fill_set = sem("inits_out"), sem("fill_set")
            block = c0.enter_context(nc.Block())

            @block.sync
            def _(sp):
                for i, w in enumerate((wq, wk, wv)):
                    sp.dma_start(wl[:, 2 * i:2 * i + 2, :], w.rearrange("(c p) f -> p c f", p=P)).then_inc(weights_in, 16)
                sp.dma_start(wol[:, :], wo).then_inc(weights_in, 16)
                for i, b in enumerate((bq, bk, bv)):
                    sp.dma_start(bias[:, i, :], b.unsqueeze(0).to_broadcast([P, HD])).then_inc(bias_in, 16)
                sp.dma_start(bob[:, :], bo.unsqueeze(0).to_broadcast([P, D])).then_inc(bias_in, 16)

                def load_x(t, par, rows):
                    sp.dma_start(xin[0:rows, par, :], x[bass.ds(t * P, rows), :]).then_inc(x_in[par], 16)

                def store_qkv(t, par):
                    sp.wait_ge(qkv_biased, t + 1)
                    sp.sem_inc(pass_sp, 1)
                    sp.dma_start(q_tab[bass.ds(t * P, P), :], qkv[:, par, 0:HD]).then_inc(qkv_out[par], 16)
                    sp.dma_start(kv_tab[bass.ds(t * P, P), :], qkv[:, par, HD:]).then_inc(qkv_out[par], 16)

                sp.wait_ge(pads_set, 1)
                load_x(0, 0, P)
                load_x(1, 1, P)
                with sp.Fori(0, NT // 2 - 1) as i:
                    for par in range(2):
                        store_qkv(2 * i + par, par)
                        load_x(2 * i + par + 2, par, P)
                store_qkv(NT - 3, 0)
                load_x(NT - 1, 0, TAIL)
                store_qkv(NT - 2, 1)
                store_qkv(NT - 1, 0)
                sp.wait_ge(qkv_out[0], 32 * (NT // 2 + 1))
                sp.wait_ge(qkv_out[1], 32 * (NT // 2))

            @block.gpsimd
            def _(gp):
                gp.memset(ident[:, :], 0.0).then_inc(pads_gp := sem("pads_gp"), 1)
                gp.memset(below[:, :], 1.0).then_inc(pads_gp, 1)
                gp.memset(above[:, :], 1.0).then_inc(pads_gp, 1)
                gp.iota(part_i[:, :], pattern=[[0, 1]], base=0, channel_multiplier=1).then_inc(consts, 1)
                gp.iota(iota_row_i[:, :], pattern=[[1, KCOLS]], base=0, channel_multiplier=0).then_inc(consts, 1)
                gp.wait_ge(pads_gp, 3)
                gp.affine_select(out=ident[:, :], in_=ident[:, :], compare_op=ALU.not_equal, fill=1.0,
                                 base=0, pattern=[[-1, P]], channel_multiplier=1).then_inc(consts, 1)
                gp.affine_select(out=below[:, :], in_=below[:, :], compare_op=ALU.is_gt, fill=0.0,
                                 base=0, pattern=[[-1, P]], channel_multiplier=1).then_inc(consts, 1)
                gp.affine_select(out=above[:, :], in_=above[:, :], compare_op=ALU.is_gt, fill=0.0,
                                 base=0, pattern=[[1, P]], channel_multiplier=-1).then_inc(consts, 1)
                with nc.allow_non_contiguous_dma(reason="768 elements, once"):
                    for k in range(KINDS):
                        gp.dma_start(embt[:, k, :], emb[k, :].rearrange("(c p) -> p c", p=P)).then_inc(emb_in, 16)

            @block.scalar
            def _(act):
                act.wait_ge(fill_set, 1)
                act.dma_start(rec.rearrange("(p s) f -> p (s f)", p=P), fill[:, 0:NS * SUP * 2 // P]).then_inc(inits_out, 16)
                act.wait_ge(fill_set, 2)
                nfull = TROWS // P
                act.dma_start(sums[0:nfull * P, :].rearrange("(t p) d -> p t d", p=P),
                              zero[:, :].unsqueeze(1).to_broadcast([P, nfull, D])).then_inc(inits_out, 16)
                act.dma_start(sums[nfull * P:TROWS, :], zero[0:TROWS - nfull * P, :]).then_inc(inits_out, 16)

                def copy_xt(t, par):
                    act.wait_ge(x_turned, t + 1)
                    act.activation(xt[:, par, :], px[:, par, 0:P], ACT.Copy).then_inc(xt_copied, 1)

                with act.Fori(0, NT // 2) as i:
                    for par in range(2):
                        copy_xt(2 * i + par, par)
                copy_xt(NT - 1, 0)
                act.wait_ge(inits_out, 48)

            @block.tensor
            def _(pe):
                pe.wait_ge(consts, 5)
                pe.wait_ge(weights_in, 64)
                for c in range(6):
                    last = pe.transpose(pw[:, c * P:(c + 1) * P], wl[:, c, :], ident[:, :])
                last.then_inc(wt_done, 1)
                pe.wait_ge(wt_copied, 1)
                for h in range(H):
                    for q in range(4):
                        last = pe.matmul(pw[32 * q:32 * q + 32, h * D:(h + 1) * D], wol[:, h * DH:(h + 1) * DH],
                                         ident[:, :], start=True, stop=True)
                last.then_inc(wo_done, 1)
                pe.wait_ge(wo_copied, 1)
                for c in range(2):
                    last = pe.transpose(pw[:, c * P:(c + 1) * P], wol[:, c * P:(c + 1) * P], ident[:, :])
                last.then_inc(wo_done, 1)
                pe.wait_ge(wo_copied, 2)
                pe.wait_ge(emb_in, 16 * KINDS)
                for k in range(KINDS):
                    for c in range(2):
                        last = pe.matmul(pw[:, k * D:(k + 1) * D], embt[:, k, c:c + 1].to_broadcast([P, P]),
                                         wot[:, c, :], start=(c == 0), stop=(c == 1))
                last.then_inc(kindw_done, 1)

                def tile(t, par, early):
                    pe.wait_ge(x_in[par], 16 * (t // 2 + 1) if isinstance(t, int) else 8 * (t - par) + 16)
                    if not early:
                        pe.wait_ge(qkv_biased, t - 1)
                    pe.transpose(px[:, par, 0:P], xin[:, par, :], ident[:, :]).then_inc(x_turned, 1)
                    pe.wait_ge(xt_copied, t + 1)
                    for c in range(2):
                        last = pe.matmul(pq[:, par, c, 0:HALF], xt[:, par, :], wt[:, c * HALF:(c + 1) * HALF],
                                         start=True, stop=True)
                    last.then_inc(qkv_done, 1)

                tile(0, 0, True)
                tile(1, 1, True)
                with pe.Fori(1, NT // 2) as i:
                    for par in range(2):
                        tile(2 * i + par, par, False)
                tile(NT - 1, 0, False)

            @block.vector
            def _(dve):
                chain = [0]

                def link(ins):
                    chain[0] += 1
                    ins.then_inc(DCH, 1)
                    dve.wait_ge(DCH, chain[0])

                dve.memset(xin[:, :, :], 0.0).then_inc(pads_set, 1)
                dve.memset(fill, PADKEY).then_inc(fill_set, 1)
                dve.memset(zero[:, :], 0.0).then_inc(fill_set, 1)
                dve.wait_ge(consts, 5)
                link(dve.tensor_copy(iota_row[:, :], iota_row_i[:, :]))
                link(dve.tensor_copy(part_f[:, :], part_i[:, :]))
                link(dve.tensor_scalar(blk_i[:, :], part_i[:, :], 3, 3, ALU.logical_shift_right, ALU.bitwise_and))
                link(dve.tensor_copy(blk_f[:, :], blk_i[:, :]))
                link(dve.tensor_scalar(own[:, :], iota_row[:, 0:BPT], blk_f[:, 0:1], None, ALU.is_equal))
                link(dve.tensor_scalar(trash[:, :], part_f[:, :], float(N), None, ALU.add))
                dve.wait_ge(wt_done, 1)
                dve.tensor_copy(wt[:, :], pw[:, 0:6 * P]).then_inc(wt_copied, 1)
                dve.wait_ge(wo_done, 1)
                dve.tensor_copy(wo4[:, :, :].rearrange("p h d -> p (h d)"), pw[:, :]).then_inc(wo_copied, 1)
                dve.wait_ge(wo_done, 2)
                dve.tensor_copy(wot[:, :, :].rearrange("p c d -> p (c d)"), pw[:, 0:2 * D]).then_inc(wo_copied, 1)
                dve.wait_ge(kindw_done, 1)
                dve.wait_ge(bias_in, 64)
                for k in range(KINDS):
                    link(dve.tensor_tensor(kindw[:, k, :], pw[:, k * D:(k + 1) * D], bob[:, :], ALU.add))
                dve.sem_clear(DCH)

                def add_bias(t, par, first):
                    dve.wait_ge(qkv_done, t + 1)
                    if not first:
                        dve.wait_ge(qkv_out[par], 32 * (t // 2) if isinstance(t, int) else 16 * (t - par))
                    dve.tensor_tensor(qkv[:, par, :].rearrange("p (c n) -> p c n", c=2), pq[:, par, :, 0:HALF],
                                      bias[:, :, :].rearrange("p a b -> p (a b)").rearrange("p (c n) -> p c n", c=2),
                                      ALU.add).then_inc(qkv_biased, 1)

                add_bias(0, 0, True)
                add_bias(1, 1, True)
                with dve.Fori(1, NT // 2) as i:
                    for par in range(2):
                        add_bias(2 * i + par, par, False)
                add_bias(NT - 1, 0, False)

        with ExitStack() as c1:
            raw = [sb(f"raw_{n}", [P, 13, P], I32, c1) for n in ("key", "dst", "kind")]
            CH = -(-ET // P)
            REM = ET - (CH - 1) * P
            FR = EFULL - (CH - 1) * P
            rawf = sb("rawf", [P, 2, P], FP32, c1)
            coli = sb("coli", [P, ET], I32, c1)
            colj = sb("colj", [P, ET], I32, c1)
            win = sb("win", [P, 2, 2, GT], FP32, c1)
            oh_lo = sb("oh_lo", [P, 2, GT, P], BF16, c1)
            oh_kh = sb("oh_kh", [P, 2, GT, KCOLS], BF16, c1)
            zero_bf = sb("zero_bf", [P, KCOLS], BF16, c1)
            total = sb("total", [P, HI], FP32, c1)
            tot_i = sb("tot_i", [P, HI], I32, c1)
            ones = sb("ones", [P, HI], FP32, c1)
            scan = sb("scan", [P, HI], FP32, c1)
            pt = c1.enter_context(nc.psum_tensor("pt", [P, 2, 512], FP32))
            hist = c1.enter_context(nc.psum_tensor("hist", [P, 512], FP32))
            pre = c1.enter_context(nc.psum_tensor("pre", [P, 512], FP32))

            pads1, edges_in, rows_out = sem("pads1"), sem("edges_in"), sem("rows_out")
            raw_f, turned, cols_done = sem("raw_f"), sem("turned"), sem("cols_done")
            onehots, counted, row_tot, prefixed = sem("onehots"), sem("counted"), sem("row_tot"), sem("prefixed")
            block = c1.enter_context(nc.Block())

            @block.sync
            def _(sp):
                sp.wait_ge(pads1, 3)
                for r, a in zip(raw, (src, dst, kind)):
                    sp.dma_start(r[:, 0:CH - 1, :], a[0:(CH - 1) * P * P].rearrange("(c q e) -> q c e", q=P, e=P)).then_inc(edges_in, 16)
                    sp.dma_start(r[0:FR, CH - 1, :], a[(CH - 1) * P * P:EFULL * P].rearrange("(q e) -> q e", e=P)).then_inc(edges_in, 16)
                    sp.dma_start(r[FR:FR + 1, CH - 1, 0:E - EFULL * P], a[EFULL * P:E].unsqueeze(0)).then_inc(edges_in, 16)
                sp.wait_ge(edges_in, 16 * 9)
                sp.dma_start(key_rows[0:(CH - 1) * P, :].rearrange("(c q) e -> q c e", q=P), raw[0][:, 0:CH - 1, :]).then_inc(rows_out, 16)
                sp.dma_start(key_rows[(CH - 1) * P:ET, :], raw[0][0:REM, CH - 1, :]).then_inc(rows_out, 16)
                sp.wait_ge(rows_out, 32)

            @block.tensor
            def _(pe):
                n = 0
                for a in range(3):
                    for c in range(CH):
                        m = P if c < CH - 1 else REM
                        pe.wait_ge(raw_f, n + 1)
                        if n >= 2:
                            pe.wait_ge(cols_done, n - 1)
                        pe.transpose(pt[:, n % 2, 0:m], rawf[0:m, n % 2, :], ident[0:m, 0:m]).then_inc(turned, 1)
                        n += 1
                pe.wait_ge(onehots, 1)
                pe.matmul(hist[:, 0:KCOLS], zero_bf[:, 0:P], zero_bf[:, :], start=True, stop=False, skip_group_check=True)

                def count(g, par):
                    pe.wait_ge(onehots, g + 1)
                    for k in range(GT):
                        last = pe.matmul(hist[:, 0:KCOLS], oh_lo[:, par, k, :], oh_kh[:, par, k, :],
                                         start=False, stop=False, skip_group_check=True)
                    last.then_inc(counted, 1)

                with pe.Fori(0, GROUPS // 2) as i:
                    for par in range(2):
                        count(2 * i + par, par)
                pe.wait_ge(row_tot, 1)
                pe.matmul(pre[:, 0:1], above[:, :], scan[:, NT - 1:NT], start=True, stop=True).then_inc(prefixed, 1)

            @block.vector
            def _(dve):
                chain = [0]

                def link(ins):
                    chain[0] += 1
                    ins.then_inc(DCH, 1)
                    dve.wait_ge(DCH, chain[0])

                for r, pad in zip(raw, (PADKEY, PADKEY, KINDS)):
                    dve.memset(r[:, CH - 1, :], pad).then_inc(pads1, 1)
                dve.memset(zero_bf[:, :], 0.0)
                dve.memset(ones[:, :], 1.0)
                dve.wait_ge(edges_in, 16 * 9)
                blocks = [(a, c) for a in range(3) for c in range(CH)]

                def to_float(n):
                    a, c = blocks[n]
                    if n >= 2:
                        dve.wait_ge(turned, n - 1)
                    m = P if c < CH - 1 else REM
                    dve.tensor_copy(rawf[0:m, n % 2, :], raw[a][0:m, c, :]).then_inc(raw_f, 1)

                to_float(0)
                for n, (a, c) in enumerate(blocks):
                    if n + 1 < len(blocks):
                        to_float(n + 1)
                    m = P if c < CH - 1 else REM
                    dve.wait_ge(turned, n + 1)
                    dve.tensor_copy((key_c, dst_c, cid_c)[a][:, c * P:c * P + m], pt[:, n % 2, 0:m]).then_inc(cols_done, 1)
                dve.wait_ge(cols_done, len(blocks))
                link(dve.tensor_copy(coli[:, :], key_c[:, :]))
                link(dve.tensor_scalar(colj[:, :], coli[:, :], P - 1, None, ALU.bitwise_and))
                link(dve.tensor_copy(lo_c[:, :], colj[:, :]))
                link(dve.tensor_scalar(colj[:, :], coli[:, :], 7, None, ALU.logical_shift_right))
                link(dve.tensor_copy(hi_c[:, :], colj[:, :]))
                link(dve.scalar_tensor_tensor(cid_c[:, :], cid_c[:, :], float(NT), hi_c[:, :], ALU.mult, ALU.add))
                dve.sem_clear(DCH)

                def onehot(g, par, first):
                    dve.tensor_copy(win[:, par, 0, :], lo_c[:, bass.ds(g * GT, GT)])
                    dve.tensor_copy(win[:, par, 1, :], cid_c[:, bass.ds(g * GT, GT)]).then_inc(DCH, 1)
                    dve.wait_ge(DCH, par + 1)
                    if not first:
                        dve.wait_ge(counted, g - 1)
                    for k in range(GT):
                        dve.tensor_scalar(oh_lo[:, par, k, :], iota_row[:, 0:P], win[:, par, 0, k:k + 1], None, ALU.is_equal)
                        last = dve.tensor_scalar(oh_kh[:, par, k, :], iota_row[:, :], win[:, par, 1, k:k + 1], None, ALU.is_equal)
                    last.then_inc(onehots, 1)

                onehot(0, 0, True)
                onehot(1, 1, True)
                dve.sem_clear(DCH)
                with dve.Fori(1, GROUPS // 2) as i:
                    for par in range(2):
                        onehot(2 * i + par, par, False)
                    dve.sem_clear(DCH)
                dve.wait_ge(counted, GROUPS)
                chain[0] = 0
                link(dve.tensor_copy(counts[:, :, :].rearrange("p k h -> p (k h)"), hist[:, 0:KCOLS]))
                link(dve.memset(total[:, :], 0.0))
                link(dve.tensor_tensor(total[:, 0:NT], counts[:, 0, :], counts[:, 1, :], ALU.add))
                link(dve.tensor_tensor(total[:, 0:NT], total[:, 0:NT], counts[:, 2, :], ALU.add))
                link(dve.tensor_scalar(total[:, 0:NT], total[:, 0:NT], float(SLOTS - 1), None, ALU.add))
                link(dve.tensor_copy(tot_i[:, :], total[:, :]))
                link(dve.tensor_scalar(tot_i[:, :], tot_i[:, :], 3, 3, ALU.logical_shift_right, ALU.logical_shift_left))
                link(dve.tensor_copy(total[:, :], tot_i[:, :]))
                link(dve.tensor_tensor_scan(scan[:, :], ones[:, :], total[:, :], 0.0, ALU.mult, ALU.add))
                dve.tensor_copy(part_f[:, :], part_i[:, :]).then_inc(row_tot, 1)
                link(dve.tensor_tensor(total[:, :], scan[:, :], total[:, :], ALU.subtract))
                dve.wait_ge(prefixed, 1)
                link(dve.tensor_scalar(first_slot[:, :], total[:, :], pre[:, 0:1], None, ALU.add))
                dve.sem_clear(DCH)

        with ExitStack() as c2:
            krow = sb("krow", [P, 2, GT * P], I32, c2)
            lrow = sb("lrow", [P, GT * P], I32, c2)
            win2 = sb("win2", [P, 2, 4, GT], FP32, c2)
            oh_e = sb("oh_e", [P, 2, GT, P], BF16, c2)
            oh_h = sb("oh_h", [P, 2, GT, HI], BF16, c2)
            oh_t = sb("oh_t", [P, 2, GT, P], FP32, c2)
            taken = sb("taken", [P, 2, HI], FP32, c2)
            junk = sb("junk", [P, GT, P], FP32, c2)
            junk_s = sb("junk_s", [P, GT, HI], FP32, c2)
            junk_p = sb("junk_p", [P, 1], FP32, c2)
            within = sb("within", [P, 2, GT], FP32, c2)
            base = sb("base", [P, 2, GT], FP32, c2)
            sl = sb("sl", [P, GT], FP32, c2)
            sli = sb("sli", [P, 4, GT], I32, c2)
            recs = sb("recs", [P, 2, GT, 2], I32, c2)
            place = sb("place", [P, 2, GT], I32, c2)
            free_slot = c2.enter_context(nc.psum_tensor("free_slot", [P, 512], FP32))
            look = c2.enter_context(nc.psum_tensor("look", [P, 4, 512], FP32))

            krow_in = [sem("krow_in0"), sem("krow_in1")]
            krow_read, ohs, tallied, snapped = sem("krow_read"), sem("ohs"), sem("tallied"), sem("snapped")
            looked, selected, placed = sem("looked"), sem("selected"), sem("placed")
            scattered = [sem("scattered0"), sem("scattered1")]
            block = c2.enter_context(nc.Block())

            @block.sync
            def _(sp):
                def load(g, par, first):
                    if not first:
                        sp.wait_ge(krow_read, g - 1)
                        sp.sem_inc(pass_sp, 1)
                    sp.dma_start(krow[:, par, :], key_rows[bass.ds(g * GT, GT), :].rearrange("t e -> (t e)")
                                 .unsqueeze(0).to_broadcast([P, GT * P])).then_inc(krow_in[par], 16)

                load(0, 0, True)
                load(1, 1, True)
                with sp.Fori(1, GROUPS // 2) as i:
                    for par in range(2):
                        load(2 * i + par, par, False)

            @block.gpsimd
            def _(gp):
                def scatter(g, par):
                    gp.wait_ge(placed, g + 1)
                    gp.sem_inc(pass_pool, 1)
                    for k in range(GT):
                        gp.indirect_dma_start(out=rec, out_offset=bass.IndirectOffsetOnAxis(ap=place[:, par, k:k + 1].bitcast(U32), axis=0),
                                              in_=recs[:, par, k, :], in_offset=None, bounds_check=NS * SUP - 1,
                                              oob_is_err=False).then_inc(scattered[par], 16)

                with gp.Fori(0, GROUPS // 2) as i:
                    for par in range(2):
                        scatter(2 * i + par, par)
                for par in range(2):
                    gp.wait_ge(scattered[par], 16 * ET // 2)

            @block.scalar
            def _(act):
                def snap(t, k, first):
                    act.wait_ge(tallied, t + 1)
                    if not first:
                        act.wait_ge(looked, t - 1)
                    act.activation(taken[:, k % 2, :], free_slot[:, 0:HI], ACT.Copy).then_inc(snapped, 1)

                for k in range(2):
                    snap(k, k, True)
                for k in range(2, 2 * GT):
                    snap(k, k, False)
                with act.Fori(1, GROUPS // 2) as i:
                    for k in range(2 * GT):
                        snap(2 * GT * i + k, k, False)

            @block.tensor
            def _(pe):
                pe.matmul(free_slot[:, 0:HI], ident[:, :], first_slot[:, :], start=True, stop=False,
                          skip_group_check=True).then_inc(tallied, 1)

                def tile(g, t, par, k, first):
                    if k == 0:
                        pe.wait_ge(ohs, g + 1)
                    pe.wait_ge(snapped, t + 1)
                    pe.matmul(free_slot[:, 0:HI], oh_e[:, par, k, :], oh_h[:, par, k, :], start=False, stop=False,
                              skip_group_check=True).then_inc(tallied, 1)
                    if not first:
                        pe.wait_ge(selected, t - 3)
                    pe.matmul(look[:, k % 4, 0:HI], oh_t[:, par, k, :], taken[:, k % 2, :], start=True,
                              stop=True).then_inc(looked, 1)

                for k in range(2 * GT):
                    tile(k // GT, k, k // GT, k % GT, k < 4)
                with pe.Fori(1, GROUPS // 2) as i:
                    for k in range(2 * GT):
                        tile(2 * i + k // GT, 2 * GT * i + k, k // GT, k % GT, False)

            @block.vector
            def _(dve):
                chain = [0]

                def link(ins):
                    chain[0] += 1
                    ins.then_inc(DCH, 1)
                    dve.wait_ge(DCH, chain[0])

                def step(g, par, do_oh, do_sel, gs=None, early=False):
                    q = 1 - par
                    if do_oh:
                        for n, a in enumerate((key_c, dst_c, lo_c, hi_c)):
                            last = dve.tensor_copy(win2[:, par, n, :], a[:, bass.ds(g * GT, GT)])
                        link(last)
                        dve.wait_ge(krow_in[par], 16 * (g // 2 + 1) if isinstance(g, int) else 8 * (g - par) + 16)
                        link(dve.tensor_scalar(lrow[:, :], krow[:, par, :], P - 1, None, ALU.bitwise_and))
                    for k in range(GT):
                        if do_oh:
                            dve.tensor_scalar(oh_e[:, par, k, :], iota_row[:, 0:P], win2[:, par, 2, k:k + 1], None, ALU.is_equal)
                            dve.tensor_scalar(oh_h[:, par, k, :], iota_row[:, 0:HI], win2[:, par, 3, k:k + 1], None, ALU.is_equal)
                            last = dve.tensor_scalar(oh_t[:, par, k, :], lrow[:, k * P:(k + 1) * P], part_f[:, 0:1], None, ALU.is_equal)
                            if k == GT - 1:
                                last.then_inc(ohs, 1)
                            last = dve.scalar_tensor_tensor(junk[:, k, :], krow[:, par, k * P:(k + 1) * P], win2[:, par, 0, k:k + 1],
                                                            below[:, :], ALU.is_equal, ALU.mult, accum_out=within[:, par, k:k + 1])
                            if k == GT - 1:
                                last.then_inc(krow_read, 1)
                        if do_sel:
                            dve.wait_ge(looked, gs * GT + k + 1)
                            last = dve.scalar_tensor_tensor(junk_s[:, k, :], iota_row[:, 0:HI], win2[:, q, 3, k:k + 1],
                                                            look[:, k % 4, 0:HI], ALU.is_equal, ALU.mult,
                                                            accum_out=base[:, q, k:k + 1])
                            last.then_inc(selected, 1)
                    if do_sel:
                        dve.wait_ge(selected, gs * GT + GT)
                        link(dve.tensor_tensor(sl[:, :], base[:, q, :], within[:, q, :], ALU.add))
                        if not early:
                            dve.wait_ge(scattered[q], (GT * 16) * (gs // 2) if isinstance(gs, int) else (GT * 8) * (gs - q))
                        link(dve.tensor_copy(sli[:, 0, :], sl[:, :]))
                        link(dve.tensor_scalar(sli[:, 1, :], sli[:, 0, :], 31, 3, ALU.bitwise_and, ALU.logical_shift_left))
                        link(dve.tensor_scalar(sli[:, 2, :], sli[:, 0, :], 5, 7, ALU.logical_shift_right, ALU.bitwise_and))
                        link(dve.tensor_scalar(sli[:, 3, :], sli[:, 0, :], 8, 8, ALU.logical_shift_right, ALU.logical_shift_left))
                        link(dve.tensor_tensor(sli[:, 1, :], sli[:, 1, :], sli[:, 2, :], ALU.bitwise_or))
                        dve.tensor_copy(recs[:, q, :, 0], win2[:, q, 1, :])
                        dve.tensor_copy(recs[:, q, :, 1], win2[:, q, 0, :])
                        link(dve.tensor_tensor(place[:, q, :], sli[:, 1, :], sli[:, 3, :], ALU.bitwise_or))
                        dve.tensor_copy(junk_p[:, :], sl[:, 0:1]).then_inc(placed, 1)
                    dve.sem_clear(DCH)
                    chain[0] = 0

                step(0, 0, True, False)
                step(1, 1, True, True, 0, True)
                step(2, 0, True, True, 1, True)
                step(3, 1, True, True, 2)
                with dve.Fori(2, GROUPS // 2) as i:
                    for par in range(2):
                        step(2 * i + par, par, True, True, 2 * i + par - 1)
                step(GROUPS, 0, False, True, GROUPS - 1)

        with ExitStack() as c3:
            slot_rec = sb("slot_rec", [P, 2, TPS, 2], I32, c3)
            blk_src = sb("blk_src", [P, 2, 1], I32, c3)
            src_f = sb("src_f", [P, 2, 1], FP32, c3)
            qg = sb("qg", [P, 2, HD], FP32, c3)
            qt = sb("qt", [P, 2, TPS, H, BPT], FP32, c3)
            valid = sb("valid", [P, TPS], FP32, c3)
            mask = sb("mask", [P, 2, TPS, BPT], FP32, c3)
            kt = sb("kt", [P, 2, BT * HD], FP32, c3)
            sc = sb("sc", [P, BT * HD], FP32, c3)
            se = sb("se", [P, BT, H, H], FP32, c3)
            ex = sb("ex", [P, BT, H, H], FP32, c3)
            mx = sb("mx", [P, BT, H], FP32, c3)
            den = sb("den", [P, BT, H], FP32, c3)
            rm = sb("rm", [P, BT, H, BPT], FP32, c3)
            at = sb("at", [P, 2, BT, H, H * BPT], FP32, c3)
            ot = sb("ot", [P, 2, H, TPS, BPT], FP32, c3)
            msg = sb("msg", [P, 2, D], FP32, c3)
            same = sb("same", [P, 2, P], FP32, c3)
            early_n = sb("early_n", [P, 1], FP32, c3)
            keep = sb("keep", [P, 2], FP32, c3)
            junk3 = sb("junk3", [P, P], FP32, c3)
            row_f = sb("row_f", [P, 1], FP32, c3)
            row_i = sb("row_i", [P, 2, 1], I32, c3)
            summed = sb("summed", [P, 2, D], FP32, c3)
            ps = c3.enter_context(nc.psum_tensor("ps", [P, 2, BT * HD], FP32))
            po = c3.enter_context(nc.psum_tensor("po", [P, 2, 512], FP32))
            pm = c3.enter_context(nc.psum_tensor("pm", [P, 512], FP32))
            pe_b = c3.enter_context(nc.psum_tensor("pe_b", [P, 512], FP32))

            rec_in = [sem("rec_in0"), sem("rec_in1")]
            q_in = [sem("q_in0"), sem("q_in1")]
            kv_in = [sem(f"kv_in{i}") for i in range(4)]
            added = sem("added")
            kv_clear = sem("kv_clear")
            q_turned, k_turned, masked, scored = sem("q_turned"), sem("k_turned"), sem("masked"), sem("scored")
            shifted, exped, weighed, valued = sem("shifted"), sem("exped"), sem("weighed"), sem("valued")
            src_floated, src_rowed, same_built = sem("src_floated"), sem("src_rowed"), sem("same_built")
            ot_copied, projected, msg_copied, blocks_summed, summed_copied = (
                sem("ot_copied"), sem("projected"), sem("msg_copied"), sem("blocks_summed"), sem("summed_copied"))
            block = c3.enter_context(nc.Block())

            def supertiles(eng, body):
                for s in range(4):
                    body(s, s % 2)
                with eng.Fori(2, NS // 2) as i:
                    for par in range(2):
                        body(2 * i + par, par)
                for s in range(NS // 2 * 2, NS + 2):
                    body(s, s % 2)

            def has(s, lag):
                return not isinstance(s, int) or 0 <= s - lag < NS

            def half(s, par):
                return (s - par) // 2 if isinstance(s, int) else s - par

            @block.sync
            def _(sp):
                def load(s, par):
                    if not has(s, 0):
                        return
                    if has(s, 2):
                        sp.wait_ge(valued, 2 * s - 2)
                        sp.sem_inc(pass_sp, 1)
                        sp.wait_ge(same_built, s - 1)
                        sp.sem_inc(pass_sp, 1)
                    sp.dma_start(slot_rec[:, par, :, :].rearrange("p j f -> p (j f)"),
                                 rec[bass.ds(s * SUP, SUP), :].rearrange("(p j) f -> p (j f)", p=P)).then_inc(rec_in[par], 16)
                    view = rec[bass.ds(s * SUP, SUP), 1].rearrange("(q b o j) -> q b o j", q=4, b=BPT, o=SLOTS)[:, :, 0, :]
                    with nc.allow_non_contiguous_dma(reason="one source a block"):
                        for q in range(4):
                            sp.dma_start(blk_src[32 * q:32 * q + 32, par, :],
                                         view[q].rearrange("b j -> j b").unsqueeze(2)).then_inc(rec_in[par], 16)

                supertiles(sp, load)

            @block.gpsimd
            def _(gp):
                gp.wait_ge(kv_clear, 1)
                def body(s, par):
                    if has(s, 0):
                        sp_val = 80 * (s // 2 + 1) if isinstance(s, int) else 40 * (s - par) + 80
                        gp.wait_ge(rec_in[par], sp_val)
                        gp.sem_inc(pass_pool, 1)
                        if has(s, 2):
                            gp.wait_ge(q_turned, s - 1)
                            gp.sem_inc(pass_pool, 1)
                        gp.indirect_dma_start(out=qg[:, par, :], out_offset=None, in_=q_tab,
                                              in_offset=bass.IndirectOffsetOnAxis(ap=blk_src[:, par, :].bitcast(U32), axis=0),
                                              bounds_check=N - 1, oob_is_err=False).then_inc(q_in[par], 16)
                        for b in range(2):
                            r = 2 * par + b
                            if has(s, 2):
                                gp.wait_ge(valued, 2 * s + b - 3)
                                gp.sem_inc(pass_pool, 1)
                            for i in range(BT):
                                gp.indirect_dma_start(out=kv[:, r, i, :], out_offset=None, in_=kv_tab,
                                                      in_offset=bass.IndirectOffsetOnAxis(
                                                          ap=slot_rec[:, par, BT * b + i, 0:1].bitcast(U32), axis=0),
                                                      bounds_check=N - 1, oob_is_err=False).then_inc(kv_in[r], 16)
                    if has(s, 2):
                        gp.wait_ge(summed_copied, s - 1)
                        gp.sem_inc(pass_pool, 1)
                        if has(s, 3):
                            gp.wait_ge(added, 16 * (s - 2))
                            gp.sem_inc(pass_pool, 1)
                        gp.indirect_dma_start(out=sums, out_offset=bass.IndirectOffsetOnAxis(ap=row_i[:, par, :].bitcast(U32), axis=0),
                                              in_=summed[:, par, :], in_offset=None, bounds_check=TROWS - 1,
                                              oob_is_err=True, compute_op=ALU.add).then_inc(added, 16)

                supertiles(gp, body)
                gp.wait_ge(added, 16 * NS)

            @block.scalar
            def _(act):
                def exp(n):
                    act.wait_ge(shifted, n + 1)
                    if not isinstance(n, int) or n >= 1:
                        act.wait_ge(weighed, n)
                    act.activation(ex[:, :, :, :].rearrange("p a g h -> p (a g h)"),
                                   se[:, :, :, :].rearrange("p a g h -> p (a g h)"), ACT.Exp, scale=SCALE).then_inc(exped, 1)

                def body(s, par):
                    if has(s, 1):
                        exp(2 * s - 1)
                    if has(s, 2):
                        act.wait_ge(projected, s - 1)
                        if has(s, 4):
                            act.wait_ge(blocks_summed, s - 3)
                        act.activation(msg[:, par, :], pm[:, 0:D], ACT.Copy).then_inc(msg_copied, 1)
                    if has(s, 0):
                        exp(2 * s)
                    if has(s, 2):
                        act.wait_ge(blocks_summed, s - 1)
                        if has(s, 4):
                            act.wait_ge(added, 16 * (s - 3))
                        act.activation(summed[:, par, :], pe_b[:, 0:D], ACT.Copy).then_inc(summed_copied, 1)
                    if has(s, 1):
                        act.wait_ge(valued, 2 * s)
                        if has(s, 3):
                            act.wait_ge(projected, s - 2)
                        act.activation(ot[:, 1 - par, :, :, :].rearrange("p h j b -> p j h b"),
                                       po[:, 1 - par, 0:TPS * 32].rearrange("p (j h b) -> p j h b", j=TPS, h=H), ACT.Copy).then_inc(ot_copied, 1)

                supertiles(act, body)

            @block.tensor
            def _(pe):
                def scores(s, par, b):
                    n = 2 * s + b
                    pe.wait_ge(k_turned, n + 1)
                    pe.sem_inc(pass_pe, 1)
                    if not isinstance(n, int) or n >= 2:
                        pe.wait_ge(shifted, n - 1)
                        pe.sem_inc(pass_pe, 1)
                    for i in range(BT):
                        for q in range(4):
                            r = slice(32 * q, 32 * q + 32)
                            j = BT * b + i
                            last = pe.matmul(ps[r, b, i * HD:(i + 1) * HD], qt[r, par, j, :, :].rearrange("p h b -> p (h b)"),
                                             kt[r, b, i * HD:(i + 1) * HD], start=True, stop=True,
                                             tile_position=(32 * q, 32 * q))
                    last.then_inc(scored, 1)

                def values(s, par, b):
                    n = 2 * s + b
                    pe.wait_ge(weighed, n + 1)
                    pe.sem_inc(pass_pe, 1)
                    if b == 0 and has(s, 2):
                        pe.wait_ge(ot_copied, s - 1)
                        pe.sem_inc(pass_pe, 1)
                    for i in range(BT):
                        j = BT * b + i
                        for g in range(H):
                            for q in range(4):
                                r = slice(32 * q, 32 * q + 32)
                                last = pe.matmul(po[r, par, 32 * j:32 * j + 32],
                                                 kv[r, 2 * par + b, i, HD + g * DH:HD + (g + 1) * DH],
                                                 at[r, b, i, g, :], start=(g == 0), stop=(g == H - 1),
                                                 tile_position=(32 * q, 32 * q))
                    last.then_inc(valued, 1)

                def body(s, par):
                    if has(s, 0):
                        scores(s, par, 0)
                    if has(s, 1):
                        values(s - 1, 1 - par, 1)
                    if has(s, 2):
                        pe.wait_ge(msg_copied, s - 1)
                        pe.sem_inc(pass_pe, 1)
                        pe.wait_ge(same_built, s if has(s, 1) else NS)
                        pe.matmul(pe_b[:, 0:D], same[:, par, :], msg[:, par, :], start=True, stop=True).then_inc(blocks_summed, 1)
                    if has(s, 0):
                        scores(s, par, 1)
                        if has(s, 2):
                            pe.wait_ge(summed_copied, s - 1)
                            pe.sem_inc(pass_pe, 1)
                        pe.wait_ge(src_floated, s + 1)
                        pe.matmul(pe_b[:, 0:P], src_f[:, par, :].to_broadcast([P, P]), ident[:, :], start=True,
                                  stop=True).then_inc(src_rowed, 1)
                        values(s, par, 0)
                    if has(s, 1):
                        pe.wait_ge(ot_copied, s)
                        pe.sem_inc(pass_pe, 1)
                        if has(s, 2):
                            pe.wait_ge(msg_copied, s - 1)
                            pe.sem_inc(pass_pe, 1)
                        for h in range(H):
                            for q in range(4):
                                r = slice(32 * q, 32 * q + 32)
                                last = pe.matmul(pm[r, 0:D], ot[r, 1 - par, h, :, :].rearrange("p j b -> p (j b)"),
                                                 wo4[r, h, :], start=(h == 0), stop=(h == H - 1),
                                                 tile_position=(32 * q, 32 * q))
                        last.then_inc(projected, 1)

                supertiles(pe, body)

            @block.vector
            def _(dve):
                chain = [0]

                def link(ins):
                    chain[0] += 1
                    ins.then_inc(DCH, 1)
                    dve.wait_ge(DCH, chain[0])

                dve.memset(qg[:, :, :], 0.0)
                dve.memset(kv[:, :, :, :].rearrange("p a b c -> p (a b c)"), 0.0).then_inc(kv_clear, 1)

                def turn_k(s, par, b):
                    r = 2 * par + b
                    n = 2 * s + b
                    dve.wait_ge(kv_in[r], 64 * (s // 2 + 1) if isinstance(s, int) else 32 * (s - par) + 64)
                    if has(s, 1):
                        dve.wait_ge(scored, n - 1)
                    dve.transpose(kt[:, b, :].rearrange("p (i c) -> p i c", i=BT), kv[:, r, :, 0:HD]).then_inc(k_turned, 1)

                def shift(s, par, b):
                    n = 2 * s + b
                    dve.wait_ge(scored, n + 1)
                    link(dve.transpose(sc[:, :], ps[:, b, :]))
                    v = sc[:, :].rearrange("p (m b) -> p m b", b=BPT)
                    f = se[:, :, :, :].rearrange("p a g h -> p (a g h)")
                    if not isinstance(n, int) or n >= 1:
                        dve.wait_ge(exped, n)
                    link(dve.tensor_scalar(f, v[:, :, 0], own[:, 0:1], None, ALU.mult))
                    for k in range(1, BPT):
                        link(dve.scalar_tensor_tensor(f, v[:, :, k], own[:, k:k + 1], f, ALU.mult, ALU.add))
                    link(dve.tensor_reduce(mx[:, :, :], se[:, :, :, :].rearrange("p a g h -> p a h g"), AX.X, ALU.max))
                    dve.tensor_tensor(se[:, :, :, :], se[:, :, :, :], mx[:, :, :].unsqueeze(2).to_broadcast([P, BT, H, H]),
                                      ALU.subtract).then_inc(shifted, 1)

                def weigh(s, par, b):
                    n = 2 * s + b
                    dve.wait_ge(exped, n + 1)
                    link(dve.tensor_reduce(den[:, :, :], ex[:, :, :, :].rearrange("p a g h -> p a h g"), AX.X, ALU.add))
                    link(dve.reciprocal(den[:, :, :], den[:, :, :]))
                    link(dve.tensor_tensor(rm[:, :, :, :], den[:, :, :].unsqueeze(3).to_broadcast([P, BT, H, BPT]),
                                           mask[:, par, BT * b:BT * b + BT, :].unsqueeze(2).to_broadcast([P, BT, H, BPT]), ALU.mult))
                    if has(s, 1):
                        dve.wait_ge(valued, n - 1)
                    for i in range(BT):
                        last = dve.tensor_tensor(at[:, b, i, :, :].rearrange("p g (h b) -> p g h b", h=H),
                                                 ex[:, i, :, :].unsqueeze(3).to_broadcast([P, H, H, BPT]),
                                                 rm[:, i, :, :].unsqueeze(1).to_broadcast([P, H, H, BPT]), ALU.mult)
                    last.then_inc(weighed, 1)

                def build_same(s, par):
                    dve.wait_ge(src_rowed, s + 1)
                    dve.tensor_scalar(same[:, par, :], pe_b[:, 0:P], src_f[:, par, :], None, ALU.is_equal)
                    link(dve.scalar_tensor_tensor(junk3[:, :], pe_b[:, 0:P], src_f[:, par, :], below[:, :], ALU.is_equal,
                                                  ALU.mult, accum_out=early_n[:, :]))
                    link(dve.tensor_scalar(keep[:, 0:1], early_n[:, :], 0.0, None, ALU.is_equal))
                    link(dve.tensor_scalar(keep[:, 1:2], src_f[:, par, :], float(N), None, ALU.is_lt))
                    link(dve.tensor_tensor(keep[:, 0:1], keep[:, 0:1], keep[:, 1:2], ALU.mult))
                    link(dve.tensor_tensor(row_f[:, :], src_f[:, par, :], trash[:, :], ALU.subtract))
                    link(dve.scalar_tensor_tensor(row_f[:, :], row_f[:, :], keep[:, 0:1], trash[:, :], ALU.mult, ALU.add))
                    if has(s, 2):
                        dve.wait_ge(added, 16 * (s - 1))
                    dve.tensor_copy(row_i[:, par, :], row_f[:, :]).then_inc(same_built, 1)

                def body(s, par):
                    if has(s, 1):
                        shift(s - 1, 1 - par, 1)
                    if has(s, 0):
                        dve.wait_ge(q_in[par], 16 * (s // 2 + 1) if isinstance(s, int) else 8 * (s - par) + 16)
                        if has(s, 2):
                            dve.wait_ge(scored, 2 * s - 2)
                        dve.transpose(qt[:, par, :, :, :].rearrange("p j h b -> p h j b"),
                                      qg[:, par, :].rearrange("p (h j b) -> p h j b", h=H, j=TPS)).then_inc(q_turned, 1)
                        turn_k(s, par, 0)
                    if has(s, 1):
                        weigh(s - 1, 1 - par, 1)
                        build_same(s - 1, 1 - par)
                    if has(s, 0):
                        if has(s, 2):
                            dve.wait_ge(blocks_summed, s - 2) if has(s, 3) else None
                        dve.tensor_copy(src_f[:, par, :], blk_src[:, par, :]).then_inc(src_floated, 1)
                        link(dve.tensor_scalar(valid[:, :], slot_rec[:, par, :, 0], float(N), None, ALU.is_lt))
                        link(dve.tensor_tensor(mask[:, par, :, :], valid[:, :].unsqueeze(2).to_broadcast([P, TPS, BPT]),
                                               own[:, :].unsqueeze(1).to_broadcast([P, TPS, BPT]), ALU.mult))
                        shift(s, par, 0)
                        turn_k(s, par, 1)
                        weigh(s, par, 0)
                    dve.sem_clear(DCH)
                    chain[0] = 0

                supertiles(dve, body)

        with ExitStack() as c4:
            xs = sb("xs", [P, NT, D], FP32, c4)
            ts = kv[:, :, :, :].rearrange("p a b c -> p (a b c)")[:, 0:NT * D].rearrange("p (t d) -> p t d", d=D)
            stat = sb("stat", [P, 3, NT], FP32, c4)
            all_in, steps, squared, rooted, y_out = sem("all_in"), sem("steps"), sem("squared"), sem("rooted"), sem("y_out")
            centred, cleared, varied = sem("centred"), sem("cleared"), sem("varied")
            block = c4.enter_context(nc.Block())

            @block.sync
            def _(sp):
                sp.wait_ge(cleared, 2)
                for tab, buf in ((x, xs), (sums, ts)):
                    sp.dma_start(buf[:, 0:NT - 1, :], tab[0:(NT - 1) * P, :].rearrange("(t p) d -> p t d", p=P)).then_inc(all_in, 16)
                    sp.dma_start(buf[0:TAIL, NT - 1, :], tab[(NT - 1) * P:N, :]).then_inc(all_in, 16)
                sp.wait_ge(steps, 1)
                sp.dma_start(out[0:(NT - 1) * P, :].rearrange("(t p) d -> p t d", p=P), xs[:, 0:NT - 1, :]).then_inc(y_out, 16)
                sp.dma_start(out[(NT - 1) * P:N, :], xs[0:TAIL, NT - 1, :]).then_inc(y_out, 16)
                sp.wait_ge(y_out, 32)

            @block.scalar
            def _(act):
                act.wait_ge(centred, 1)
                act.activation(ts, xs[:, :, :], ACT.Square).then_inc(squared, 1)
                act.wait_ge(varied, 1)
                act.activation(stat[:, 1, :], stat[:, 0, :], ACT.Sqrt).then_inc(rooted, 1)

            @block.vector
            def _(dve):
                chain = [0]

                def link(ins):
                    chain[0] += 1
                    ins.then_inc(DCH, 1)
                    dve.wait_ge(DCH, chain[0])

                def per_row(a):
                    return a.unsqueeze(2).to_broadcast([P, NT, D])

                dve.memset(xs[:, NT - 1, :], 0.0).then_inc(cleared, 1)
                dve.memset(ts[:, NT - 1, :], 0.0).then_inc(cleared, 1)
                dve.wait_ge(all_in, 64)
                link(dve.tensor_tensor(xs[:, :, :], xs[:, :, :], ts, ALU.add))
                for k in range(KINDS):
                    for t in range(NT):
                        last = dve.scalar_tensor_tensor(xs[:, t, :], kindw[:, k, :], counts[:, k, t:t + 1], xs[:, t, :], ALU.mult, ALU.add)
                    link(last)
                link(dve.tensor_reduce(stat[:, 2, :], xs[:, :, :], AX.X, ALU.add))
                link(dve.tensor_scalar(stat[:, 2, :], stat[:, 2, :], 1.0 / D, None, ALU.mult))
                dve.tensor_tensor(xs[:, :, :], xs[:, :, :], per_row(stat[:, 2, :]), ALU.subtract).then_inc(centred, 1)
                dve.wait_ge(squared, 1)
                link(dve.tensor_reduce(stat[:, 2, :], ts, AX.X, ALU.add))
                dve.tensor_scalar(stat[:, 0, :], stat[:, 2, :], 1.0 / D, EPS, ALU.mult, ALU.add).then_inc(varied, 1)
                dve.wait_ge(rooted, 1)
                link(dve.reciprocal(stat[:, 2, :], stat[:, 1, :]))
                dve.tensor_tensor(xs[:, :, :], xs[:, :, :], per_row(stat[:, 2, :]), ALU.mult).then_inc(steps, 1)


_INS = ["x", "src", "dst", "edge_type_3", "L0_gnn_Wq", "L0_gnn_bq", "L0_gnn_Wk", "L0_gnn_bk", "L0_gnn_Wv", "L0_gnn_bv",
        "L0_gnn_edge_emb", "L0_gnn_Wo", "L0_gnn_bo"]


def kernel(**inputs):
    import numpy as _np
    import concourse.bacc as _bacc
    from concourse import mybir as _mybir
    from concourse.bass_utils import run_bass_kernel_spmd as _run

    nc = _bacc.Bacc("TRN2", target_bir_lowering=False, num_devices=1)
    arrays, args = {}, []
    for name in _INS:
        a = _np.ascontiguousarray(inputs[name])
        arrays[f"in_{name}_dram"] = a
        args.append(nc.dram_tensor(f"in_{name}_dram", a.shape, _mybir.dt.from_np(a.dtype), kind="ExternalInput").ap())
    args.append(nc.dram_tensor("out_0_dram", (N, D), _mybir.dt.float32, kind="ExternalOutput").ap())
    build(nc, *args)
    r = _run(nc, [arrays], core_ids=[0])
    return r.results[0]["out_0_dram"]
```

```python
import numpy as np
import concourse.bass as bass
from concourse import mybir
from contextlib import ExitStack

FP32 = mybir.dt.float32
BF16 = mybir.dt.bfloat16
I32 = mybir.dt.int32
U32 = mybir.dt.uint32
ALU = mybir.AluOpType
ACT = mybir.ActivationFunctionType
AX = mybir.AxisListType

P = 128
N = 6250
E = 200000
D = 128
HD = 256
H = 8
DH = HD // H
KINDS = 3
NT = -(-N // P)
TAIL = N - (NT - 1) * P
EPS = 1e-5
SCALE = 1.0 / float(np.sqrt(np.float32(DH)))

GT = 8
GROUPS = 2 * (-(-E // (2 * GT * P)))
ET = GROUPS * GT
EFULL = E // P
HI = NT + 1
PADKEY = NT * P + P - 1
KCOLS = KINDS * NT

SLOTS = 8
BLOCKS = (E + (SLOTS - 1) * N) // SLOTS
NS = -(-BLOCKS // P)
TPS = SLOTS
SUP = P * SLOTS
BT = 4
RB = 8
BPT = 4
TROWS = N + P


def build(nc, x, src, dst, kind, wq, bq, wk, bk, wv, bv, emb, wo, bo, out):
    with ExitStack() as ctx:
        def sb(name, shape, dt=FP32, c=ctx):
            return c.enter_context(nc.sbuf_tensor(name, shape, dt))

        def sem(name):
            return ctx.enter_context(nc.semaphore(name))

        q_tab = nc.dram_tensor("q_tab", [NT * P, HD], FP32).ap()
        kv_tab = nc.dram_tensor("kv_tab", [NT * P, 2 * HD], FP32).ap()
        key_rows = nc.dram_tensor("key_rows", [ET, P], I32).ap()
        rec = nc.dram_tensor("rec", [NS * SUP, 2], I32).ap()
        sums = nc.dram_tensor("sums", [TROWS, HD], FP32).ap()

        ident = sb("ident", [P, P])
        below = sb("below", [P, P])
        above = sb("above", [P, P])
        iota_row_i = sb("iota_row_i", [P, KCOLS], I32)
        iota_row = sb("iota_row", [P, KCOLS], BF16)
        part_i = sb("part_i", [P, 1], I32)
        part_f = sb("part_f", [P, 1])
        blk_i = sb("blk_i", [P, 1], I32)
        blk_f = sb("blk_f", [P, 1])
        own = sb("own", [P, BPT])
        trash = sb("trash", [P, 1])
        wot = sb("wot", [P, 2, D])
        perm = sb("perm", [P, P])
        kindw = sb("kindw", [P, KINDS, D])
        key_c = sb("key_c", [P, ET])
        dst_c = sb("dst_c", [P, ET])
        lo_c = sb("lo_c", [P, ET])
        hi_c = sb("hi_c", [P, ET])
        cid_c = sb("cid_c", [P, ET])
        counts = sb("counts", [P, KINDS, NT])
        first_slot = sb("first_slot", [P, HI])
        kv = sb("kv", [P, RB, BT, 2 * HD])

        DCH = sem("DCH")
        pass_sp, pass_pool, pass_pe = sem("pass_sp"), sem("pass_pool"), sem("pass_pe")

        with ExitStack() as c0:
            wl = sb("wl", [P, 6, D], FP32, c0)
            wt = sb("wt", [P, 6 * P], FP32, c0)
            bias = sb("bias", [P, 3, HD], FP32, c0)
            wol = sb("wol", [P, HD], FP32, c0)
            bob = sb("bob", [P, D], FP32, c0)
            embt = sb("embt", [P, KINDS, 2], FP32, c0)
            xin = sb("xin", [P, 2, D], FP32, c0)
            xt = sb("xt", [P, 2, P], FP32, c0)
            qkv = sb("qkv", [P, 2, 3 * HD], FP32, c0)
            zero = sb("zero", [P, HD], FP32, c0)
            fill = kv[:, :, :, :].rearrange("p a b c -> p (a b c)")[:, 0:NS * SUP * 2 // P].bitcast(I32)
            pw = c0.enter_context(nc.psum_tensor("pw", [P, 1024], FP32))
            px = c0.enter_context(nc.psum_tensor("px", [P, 2, 512], FP32))
            pq = c0.enter_context(nc.psum_tensor("pq", [P, 2, 2, 512], FP32))
            HALF = 3 * HD // 2

            weights_in, emb_in, bias_in = sem("weights_in"), sem("emb_in"), sem("bias_in")
            consts, wt_done, wo_done, wo_copied = sem("consts"), sem("wt_done"), sem("wo_done"), sem("wo_copied")
            wt_copied, kindw_done, pads_set = sem("wt_copied"), sem("kindw_done"), sem("pads_set")
            x_in = [sem("x_in0"), sem("x_in1")]
            x_turned, xt_copied, qkv_done, qkv_biased = sem("x_turned"), sem("xt_copied"), sem("qkv_done"), sem("qkv_biased")
            qkv_out = [sem("qkv_out0"), sem("qkv_out1")]
            inits_out, fill_set = sem("inits_out"), sem("fill_set")
            block = c0.enter_context(nc.Block())

            @block.sync
            def _(sp):
                for i, w in enumerate((wq, wk, wv)):
                    sp.dma_start(wl[:, 2 * i:2 * i + 2, :], w.rearrange("(c p) f -> p c f", p=P)).then_inc(weights_in, 16)
                sp.dma_start(wol[:, :], wo).then_inc(weights_in, 16)
                for i, b in enumerate((bq, bk, bv)):
                    sp.dma_start(bias[:, i, :], b.unsqueeze(0).to_broadcast([P, HD])).then_inc(bias_in, 16)
                sp.dma_start(bob[:, :], bo.unsqueeze(0).to_broadcast([P, D])).then_inc(bias_in, 16)

                def load_x(t, par, rows):
                    sp.dma_start(xin[0:rows, par, :], x[bass.ds(t * P, rows), :]).then_inc(x_in[par], 16)

                def store_qkv(t, par):
                    sp.wait_ge(qkv_biased, t + 1)
                    sp.sem_inc(pass_sp, 1)
                    sp.dma_start(q_tab[bass.ds(t * P, P), :], qkv[:, par, 0:HD]).then_inc(qkv_out[par], 16)
                    sp.dma_start(kv_tab[bass.ds(t * P, P), :], qkv[:, par, HD:]).then_inc(qkv_out[par], 16)

                sp.wait_ge(pads_set, 1)
                load_x(0, 0, P)
                load_x(1, 1, P)
                with sp.Fori(0, NT // 2 - 1) as i:
                    for par in range(2):
                        store_qkv(2 * i + par, par)
                        load_x(2 * i + par + 2, par, P)
                store_qkv(NT - 3, 0)
                load_x(NT - 1, 0, TAIL)
                store_qkv(NT - 2, 1)
                store_qkv(NT - 1, 0)
                sp.wait_ge(qkv_out[0], 32 * (NT // 2 + 1))
                sp.wait_ge(qkv_out[1], 32 * (NT // 2))

            @block.gpsimd
            def _(gp):
                gp.memset(ident[:, :], 0.0).then_inc(pads_gp := sem("pads_gp"), 1)
                gp.memset(below[:, :], 1.0).then_inc(pads_gp, 1)
                gp.memset(above[:, :], 1.0).then_inc(pads_gp, 1)
                gp.iota(part_i[:, :], pattern=[[0, 1]], base=0, channel_multiplier=1).then_inc(consts, 1)
                gp.iota(iota_row_i[:, :], pattern=[[1, KCOLS]], base=0, channel_multiplier=0).then_inc(consts, 1)
                gp.wait_ge(pads_gp, 3)
                gp.affine_select(out=ident[:, :], in_=ident[:, :], compare_op=ALU.not_equal, fill=1.0,
                                 base=0, pattern=[[-1, P]], channel_multiplier=1).then_inc(consts, 1)
                gp.affine_select(out=below[:, :], in_=below[:, :], compare_op=ALU.is_gt, fill=0.0,
                                 base=0, pattern=[[-1, P]], channel_multiplier=1).then_inc(consts, 1)
                gp.affine_select(out=above[:, :], in_=above[:, :], compare_op=ALU.is_gt, fill=0.0,
                                 base=0, pattern=[[1, P]], channel_multiplier=-1).then_inc(consts, 1)
                with nc.allow_non_contiguous_dma(reason="768 elements, once"):
                    for k in range(KINDS):
                        gp.dma_start(embt[:, k, :], emb[k, :].rearrange("(c p) -> p c", p=P)).then_inc(emb_in, 16)

            @block.scalar
            def _(act):
                act.wait_ge(fill_set, 1)
                act.dma_start(rec.rearrange("(p s) f -> p (s f)", p=P), fill).then_inc(inits_out, 16)
                act.wait_ge(fill_set, 2)
                nfull = TROWS // P
                act.dma_start(sums[0:nfull * P, :].rearrange("(t p) d -> p t d", p=P),
                              zero[:, :].unsqueeze(1).to_broadcast([P, nfull, HD])).then_inc(inits_out, 16)
                act.dma_start(sums[nfull * P:TROWS, :], zero[0:TROWS - nfull * P, :]).then_inc(inits_out, 16)

                def copy_xt(t, par):
                    act.wait_ge(x_turned, t + 1)
                    act.activation(xt[:, par, :], px[:, par, 0:P], ACT.Copy).then_inc(xt_copied, 1)

                with act.Fori(0, NT // 2) as i:
                    for par in range(2):
                        copy_xt(2 * i + par, par)
                copy_xt(NT - 1, 0)
                act.wait_ge(inits_out, 48)

            @block.tensor
            def _(pe):
                pe.wait_ge(consts, 5)
                pe.wait_ge(weights_in, 64)
                for c in range(6):
                    last = pe.transpose(pw[:, c * P:(c + 1) * P], wl[:, c, :], ident[:, :])
                last.then_inc(wt_done, 1)
                pe.wait_ge(wt_copied, 1)
                for c in range(2):
                    last = pe.transpose(pw[:, c * P:(c + 1) * P], wol[:, c * P:(c + 1) * P], ident[:, :])
                last.then_inc(wo_done, 1)
                pe.wait_ge(wo_copied, 1)
                pe.wait_ge(emb_in, 16 * KINDS)
                for k in range(KINDS):
                    for c in range(2):
                        last = pe.matmul(pw[:, k * D:(k + 1) * D], embt[:, k, c:c + 1].to_broadcast([P, P]),
                                         wot[:, c, :], start=(c == 0), stop=(c == 1))
                last.then_inc(kindw_done, 1)

                def tile(t, par, early):
                    pe.wait_ge(x_in[par], 16 * (t // 2 + 1) if isinstance(t, int) else 8 * (t - par) + 16)
                    if not early:
                        pe.wait_ge(qkv_biased, t - 1)
                    pe.transpose(px[:, par, 0:P], xin[:, par, :], ident[:, :]).then_inc(x_turned, 1)
                    pe.wait_ge(xt_copied, t + 1)
                    for c in range(2):
                        last = pe.matmul(pq[:, par, c, 0:HALF], xt[:, par, :], wt[:, c * HALF:(c + 1) * HALF],
                                         start=True, stop=True)
                    last.then_inc(qkv_done, 1)

                tile(0, 0, True)
                tile(1, 1, True)
                with pe.Fori(1, NT // 2) as i:
                    for par in range(2):
                        tile(2 * i + par, par, False)
                tile(NT - 1, 0, False)

            @block.vector
            def _(dve):
                chain = [0]

                def link(ins):
                    chain[0] += 1
                    ins.then_inc(DCH, 1)
                    dve.wait_ge(DCH, chain[0])

                dve.memset(xin[:, :, :], 0.0).then_inc(pads_set, 1)
                dve.memset(fill, PADKEY).then_inc(fill_set, 1)
                dve.memset(zero[:, :], 0.0).then_inc(fill_set, 1)
                dve.wait_ge(consts, 5)
                link(dve.tensor_copy(iota_row[:, :], iota_row_i[:, :]))
                link(dve.tensor_copy(part_f[:, :], part_i[:, :]))
                link(dve.tensor_scalar(blk_i[:, :], part_i[:, :], 3, 3, ALU.logical_shift_right, ALU.bitwise_and))
                link(dve.tensor_copy(blk_f[:, :], blk_i[:, :]))
                link(dve.tensor_scalar(own[:, :], iota_row[:, 0:BPT], blk_f[:, 0:1], None, ALU.is_equal))
                link(dve.tensor_scalar(trash[:, :], part_f[:, :], float(N), None, ALU.add))
                dve.wait_ge(wt_done, 1)
                dve.tensor_copy(wt[:, :], pw[:, 0:6 * P]).then_inc(wt_copied, 1)
                for i in range(BT):
                    last = dve.tensor_copy(perm[:, 32 * i:32 * i + 32].rearrange("p (b q k) -> p b q k", b=2, q=4),
                                           ident[:, :].rearrange("p (q b i k) -> p i b q k", q=4, b=2, i=BT)[:, i])
                link(last)
                dve.wait_ge(wo_done, 1)
                dve.tensor_copy(wot[:, :, :].rearrange("p c d -> p (c d)"), pw[:, 0:2 * D]).then_inc(wo_copied, 1)
                dve.wait_ge(kindw_done, 1)
                dve.wait_ge(bias_in, 64)
                for k in range(KINDS):
                    link(dve.tensor_tensor(kindw[:, k, :], pw[:, k * D:(k + 1) * D], bob[:, :], ALU.add))
                dve.sem_clear(DCH)

                def add_bias(t, par, first):
                    dve.wait_ge(qkv_done, t + 1)
                    if not first:
                        dve.wait_ge(qkv_out[par], 32 * (t // 2) if isinstance(t, int) else 16 * (t - par))
                    dve.tensor_tensor(qkv[:, par, :].rearrange("p (c n) -> p c n", c=2), pq[:, par, :, 0:HALF],
                                      bias[:, :, :].rearrange("p a b -> p (a b)").rearrange("p (c n) -> p c n", c=2),
                                      ALU.add).then_inc(qkv_biased, 1)

                add_bias(0, 0, True)
                add_bias(1, 1, True)
                with dve.Fori(1, NT // 2) as i:
                    for par in range(2):
                        add_bias(2 * i + par, par, False)
                add_bias(NT - 1, 0, False)

        with ExitStack() as c1:
            raw = [sb(f"raw_{n}", [P, 13, P], I32, c1) for n in ("key", "dst", "kind")]
            CH = -(-ET // P)
            REM = ET - (CH - 1) * P
            FR = EFULL - (CH - 1) * P
            rawf = sb("rawf", [P, 2, P], FP32, c1)
            coli = sb("coli", [P, ET], I32, c1)
            colj = sb("colj", [P, ET], I32, c1)
            win = sb("win", [P, 2, 2, GT], FP32, c1)
            oh_lo = sb("oh_lo", [P, 2, GT, P], BF16, c1)
            oh_kh = sb("oh_kh", [P, 2, GT, KCOLS], BF16, c1)
            zero_bf = sb("zero_bf", [P, KCOLS], BF16, c1)
            total = sb("total", [P, HI], FP32, c1)
            tot_i = sb("tot_i", [P, HI], I32, c1)
            ones = sb("ones", [P, HI], FP32, c1)
            scan = sb("scan", [P, HI], FP32, c1)
            pt = c1.enter_context(nc.psum_tensor("pt", [P, 2, 512], FP32))
            hist = c1.enter_context(nc.psum_tensor("hist", [P, 512], FP32))
            pre = c1.enter_context(nc.psum_tensor("pre", [P, 512], FP32))

            pads1, edges_in, rows_out = sem("pads1"), sem("edges_in"), sem("rows_out")
            raw_f, turned, cols_done = sem("raw_f"), sem("turned"), sem("cols_done")
            onehots, counted, row_tot, prefixed = sem("onehots"), sem("counted"), sem("row_tot"), sem("prefixed")
            block = c1.enter_context(nc.Block())

            @block.sync
            def _(sp):
                sp.wait_ge(pads1, 3)
                for r, a in zip(raw, (src, dst, kind)):
                    sp.dma_start(r[:, 0:CH - 1, :], a[0:(CH - 1) * P * P].rearrange("(c q e) -> q c e", q=P, e=P)).then_inc(edges_in, 16)
                    sp.dma_start(r[0:FR, CH - 1, :], a[(CH - 1) * P * P:EFULL * P].rearrange("(q e) -> q e", e=P)).then_inc(edges_in, 16)
                    sp.dma_start(r[FR:FR + 1, CH - 1, 0:E - EFULL * P], a[EFULL * P:E].unsqueeze(0)).then_inc(edges_in, 16)
                sp.wait_ge(edges_in, 16 * 9)
                sp.dma_start(key_rows[0:(CH - 1) * P, :].rearrange("(c q) e -> q c e", q=P), raw[0][:, 0:CH - 1, :]).then_inc(rows_out, 16)
                sp.dma_start(key_rows[(CH - 1) * P:ET, :], raw[0][0:REM, CH - 1, :]).then_inc(rows_out, 16)
                sp.wait_ge(rows_out, 32)

            @block.tensor
            def _(pe):
                n = 0
                for a in range(3):
                    for c in range(CH):
                        m = P if c < CH - 1 else REM
                        pe.wait_ge(raw_f, n + 1)
                        if n >= 2:
                            pe.wait_ge(cols_done, n - 1)
                        pe.transpose(pt[:, n % 2, 0:m], rawf[0:m, n % 2, :], ident[0:m, 0:m]).then_inc(turned, 1)
                        n += 1
                pe.wait_ge(onehots, 1)
                pe.matmul(hist[:, 0:KCOLS], zero_bf[:, 0:P], zero_bf[:, :], start=True, stop=False, skip_group_check=True)

                def count(g, par):
                    pe.wait_ge(onehots, g + 1)
                    for k in range(GT):
                        last = pe.matmul(hist[:, 0:KCOLS], oh_lo[:, par, k, :], oh_kh[:, par, k, :],
                                         start=False, stop=False, skip_group_check=True)
                    last.then_inc(counted, 1)

                with pe.Fori(0, GROUPS // 2) as i:
                    for par in range(2):
                        count(2 * i + par, par)
                pe.wait_ge(row_tot, 1)
                pe.matmul(pre[:, 0:1], above[:, :], scan[:, NT - 1:NT], start=True, stop=True).then_inc(prefixed, 1)

            @block.vector
            def _(dve):
                chain = [0]

                def link(ins):
                    chain[0] += 1
                    ins.then_inc(DCH, 1)
                    dve.wait_ge(DCH, chain[0])

                for r, pad in zip(raw, (PADKEY, PADKEY, KINDS)):
                    dve.memset(r[:, CH - 1, :], pad).then_inc(pads1, 1)
                dve.memset(zero_bf[:, :], 0.0)
                dve.memset(ones[:, :], 1.0)
                dve.wait_ge(edges_in, 16 * 9)
                blocks = [(a, c) for a in range(3) for c in range(CH)]

                def to_float(n):
                    a, c = blocks[n]
                    if n >= 2:
                        dve.wait_ge(turned, n - 1)
                    m = P if c < CH - 1 else REM
                    dve.tensor_copy(rawf[0:m, n % 2, :], raw[a][0:m, c, :]).then_inc(raw_f, 1)

                to_float(0)
                for n, (a, c) in enumerate(blocks):
                    if n + 1 < len(blocks):
                        to_float(n + 1)
                    m = P if c < CH - 1 else REM
                    dve.wait_ge(turned, n + 1)
                    dve.tensor_copy((key_c, dst_c, cid_c)[a][:, c * P:c * P + m], pt[:, n % 2, 0:m]).then_inc(cols_done, 1)
                dve.wait_ge(cols_done, len(blocks))
                link(dve.tensor_copy(coli[:, :], key_c[:, :]))
                link(dve.tensor_scalar(colj[:, :], coli[:, :], P - 1, None, ALU.bitwise_and))
                link(dve.tensor_copy(lo_c[:, :], colj[:, :]))
                link(dve.tensor_scalar(colj[:, :], coli[:, :], 7, None, ALU.logical_shift_right))
                link(dve.tensor_copy(hi_c[:, :], colj[:, :]))
                link(dve.scalar_tensor_tensor(cid_c[:, :], cid_c[:, :], float(NT), hi_c[:, :], ALU.mult, ALU.add))
                dve.sem_clear(DCH)

                def onehot(g, par, first):
                    dve.tensor_copy(win[:, par, 0, :], lo_c[:, bass.ds(g * GT, GT)])
                    dve.tensor_copy(win[:, par, 1, :], cid_c[:, bass.ds(g * GT, GT)]).then_inc(DCH, 1)
                    dve.wait_ge(DCH, par + 1)
                    if not first:
                        dve.wait_ge(counted, g - 1)
                    for k in range(GT):
                        dve.tensor_scalar(oh_lo[:, par, k, :], iota_row[:, 0:P], win[:, par, 0, k:k + 1], None, ALU.is_equal)
                        last = dve.tensor_scalar(oh_kh[:, par, k, :], iota_row[:, :], win[:, par, 1, k:k + 1], None, ALU.is_equal)
                    last.then_inc(onehots, 1)

                onehot(0, 0, True)
                onehot(1, 1, True)
                dve.sem_clear(DCH)
                with dve.Fori(1, GROUPS // 2) as i:
                    for par in range(2):
                        onehot(2 * i + par, par, False)
                    dve.sem_clear(DCH)
                dve.wait_ge(counted, GROUPS)
                chain[0] = 0
                link(dve.tensor_copy(counts[:, :, :].rearrange("p k h -> p (k h)"), hist[:, 0:KCOLS]))
                link(dve.memset(total[:, :], 0.0))
                link(dve.tensor_tensor(total[:, 0:NT], counts[:, 0, :], counts[:, 1, :], ALU.add))
                link(dve.tensor_tensor(total[:, 0:NT], total[:, 0:NT], counts[:, 2, :], ALU.add))
                link(dve.tensor_scalar(total[:, 0:NT], total[:, 0:NT], float(SLOTS - 1), None, ALU.add))
                link(dve.tensor_copy(tot_i[:, :], total[:, :]))
                link(dve.tensor_scalar(tot_i[:, :], tot_i[:, :], 3, 3, ALU.logical_shift_right, ALU.logical_shift_left))
                link(dve.tensor_copy(total[:, :], tot_i[:, :]))
                link(dve.tensor_tensor_scan(scan[:, :], ones[:, :], total[:, :], 0.0, ALU.mult, ALU.add))
                dve.tensor_copy(part_f[:, :], part_i[:, :]).then_inc(row_tot, 1)
                link(dve.tensor_tensor(total[:, :], scan[:, :], total[:, :], ALU.subtract))
                dve.wait_ge(prefixed, 1)
                link(dve.tensor_scalar(first_slot[:, :], total[:, :], pre[:, 0:1], None, ALU.add))
                dve.sem_clear(DCH)

        with ExitStack() as c2:
            krow = sb("krow", [P, 2, GT * P], I32, c2)
            lrow = sb("lrow", [P, GT * P], I32, c2)
            win2 = sb("win2", [P, 2, 4, GT], FP32, c2)
            oh_e = sb("oh_e", [P, 2, GT, P], BF16, c2)
            oh_h = sb("oh_h", [P, 2, GT, HI], BF16, c2)
            oh_t = sb("oh_t", [P, 2, GT, P], FP32, c2)
            taken = sb("taken", [P, 2, HI], FP32, c2)
            junk = sb("junk", [P, GT, P], FP32, c2)
            junk_s = sb("junk_s", [P, GT, HI], FP32, c2)
            junk_p = sb("junk_p", [P, 1], FP32, c2)
            within = sb("within", [P, 2, GT], FP32, c2)
            base = sb("base", [P, 2, GT], FP32, c2)
            sl = sb("sl", [P, GT], FP32, c2)
            sli = sb("sli", [P, 4, GT], I32, c2)
            recs = sb("recs", [P, 2, GT, 2], I32, c2)
            place = sb("place", [P, 2, GT], I32, c2)
            free_slot = c2.enter_context(nc.psum_tensor("free_slot", [P, 512], FP32))
            look = c2.enter_context(nc.psum_tensor("look", [P, 4, 512], FP32))

            krow_in = [sem("krow_in0"), sem("krow_in1")]
            krow_read, ohs, tallied, snapped = sem("krow_read"), sem("ohs"), sem("tallied"), sem("snapped")
            looked, selected, placed = sem("looked"), sem("selected"), sem("placed")
            scattered = [sem("scattered0"), sem("scattered1")]
            block = c2.enter_context(nc.Block())

            @block.sync
            def _(sp):
                def load(g, par, first):
                    if not first:
                        sp.wait_ge(krow_read, g - 1)
                        sp.sem_inc(pass_sp, 1)
                    sp.dma_start(krow[:, par, :], key_rows[bass.ds(g * GT, GT), :].rearrange("t e -> (t e)")
                                 .unsqueeze(0).to_broadcast([P, GT * P])).then_inc(krow_in[par], 16)

                load(0, 0, True)
                load(1, 1, True)
                with sp.Fori(1, GROUPS // 2) as i:
                    for par in range(2):
                        load(2 * i + par, par, False)

            @block.gpsimd
            def _(gp):
                def scatter(g, par):
                    gp.wait_ge(placed, g + 1)
                    gp.sem_inc(pass_pool, 1)
                    for k in range(GT):
                        gp.indirect_dma_start(out=rec, out_offset=bass.IndirectOffsetOnAxis(ap=place[:, par, k:k + 1].bitcast(U32), axis=0),
                                              in_=recs[:, par, k, :], in_offset=None, bounds_check=NS * SUP - 1,
                                              oob_is_err=False).then_inc(scattered[par], 16)

                with gp.Fori(0, GROUPS // 2) as i:
                    for par in range(2):
                        scatter(2 * i + par, par)
                for par in range(2):
                    gp.wait_ge(scattered[par], 16 * ET // 2)

            @block.scalar
            def _(act):
                def snap(t, k, first):
                    act.wait_ge(tallied, t + 1)
                    if not first:
                        act.wait_ge(looked, t - 1)
                    act.activation(taken[:, k % 2, :], free_slot[:, 0:HI], ACT.Copy).then_inc(snapped, 1)

                for k in range(2):
                    snap(k, k, True)
                for k in range(2, 2 * GT):
                    snap(k, k, False)
                with act.Fori(1, GROUPS // 2) as i:
                    for k in range(2 * GT):
                        snap(2 * GT * i + k, k, False)

            @block.tensor
            def _(pe):
                pe.matmul(free_slot[:, 0:HI], ident[:, :], first_slot[:, :], start=True, stop=False,
                          skip_group_check=True).then_inc(tallied, 1)

                def tile(g, t, par, k, first):
                    if k == 0:
                        pe.wait_ge(ohs, g + 1)
                    pe.wait_ge(snapped, t + 1)
                    pe.matmul(free_slot[:, 0:HI], oh_e[:, par, k, :], oh_h[:, par, k, :], start=False, stop=False,
                              skip_group_check=True).then_inc(tallied, 1)
                    if not first:
                        pe.wait_ge(selected, t - 3)
                    pe.matmul(look[:, k % 4, 0:HI], oh_t[:, par, k, :], taken[:, k % 2, :], start=True,
                              stop=True).then_inc(looked, 1)

                for k in range(2 * GT):
                    tile(k // GT, k, k // GT, k % GT, k < 4)
                with pe.Fori(1, GROUPS // 2) as i:
                    for k in range(2 * GT):
                        tile(2 * i + k // GT, 2 * GT * i + k, k // GT, k % GT, False)

            @block.vector
            def _(dve):
                chain = [0]

                def link(ins):
                    chain[0] += 1
                    ins.then_inc(DCH, 1)
                    dve.wait_ge(DCH, chain[0])

                def step(g, par, do_oh, do_sel, gs=None, early=False):
                    q = 1 - par
                    if do_oh:
                        for n, a in enumerate((key_c, dst_c, lo_c, hi_c)):
                            last = dve.tensor_copy(win2[:, par, n, :], a[:, bass.ds(g * GT, GT)])
                        link(last)
                        dve.wait_ge(krow_in[par], 16 * (g // 2 + 1) if isinstance(g, int) else 8 * (g - par) + 16)
                        link(dve.tensor_scalar(lrow[:, :], krow[:, par, :], P - 1, None, ALU.bitwise_and))
                    for k in range(GT):
                        if do_oh:
                            dve.tensor_scalar(oh_e[:, par, k, :], iota_row[:, 0:P], win2[:, par, 2, k:k + 1], None, ALU.is_equal)
                            dve.tensor_scalar(oh_h[:, par, k, :], iota_row[:, 0:HI], win2[:, par, 3, k:k + 1], None, ALU.is_equal)
                            last = dve.tensor_scalar(oh_t[:, par, k, :], lrow[:, k * P:(k + 1) * P], part_f[:, 0:1], None, ALU.is_equal)
                            if k == GT - 1:
                                last.then_inc(ohs, 1)
                            last = dve.scalar_tensor_tensor(junk[:, k, :], krow[:, par, k * P:(k + 1) * P], win2[:, par, 0, k:k + 1],
                                                            below[:, :], ALU.is_equal, ALU.mult, accum_out=within[:, par, k:k + 1])
                            if k == GT - 1:
                                last.then_inc(krow_read, 1)
                        if do_sel:
                            dve.wait_ge(looked, gs * GT + k + 1)
                            last = dve.scalar_tensor_tensor(junk_s[:, k, :], iota_row[:, 0:HI], win2[:, q, 3, k:k + 1],
                                                            look[:, k % 4, 0:HI], ALU.is_equal, ALU.mult,
                                                            accum_out=base[:, q, k:k + 1])
                            last.then_inc(selected, 1)
                    if do_sel:
                        dve.wait_ge(selected, gs * GT + GT)
                        link(dve.tensor_tensor(sl[:, :], base[:, q, :], within[:, q, :], ALU.add))
                        if not early:
                            dve.wait_ge(scattered[q], (GT * 16) * (gs // 2) if isinstance(gs, int) else (GT * 8) * (gs - q))
                        link(dve.tensor_copy(sli[:, 0, :], sl[:, :]))
                        link(dve.tensor_scalar(sli[:, 1, :], sli[:, 0, :], 31, 3, ALU.bitwise_and, ALU.logical_shift_left))
                        link(dve.tensor_scalar(sli[:, 2, :], sli[:, 0, :], 5, 7, ALU.logical_shift_right, ALU.bitwise_and))
                        link(dve.tensor_scalar(sli[:, 3, :], sli[:, 0, :], 8, 8, ALU.logical_shift_right, ALU.logical_shift_left))
                        link(dve.tensor_tensor(sli[:, 1, :], sli[:, 1, :], sli[:, 2, :], ALU.bitwise_or))
                        dve.tensor_copy(recs[:, q, :, 0], win2[:, q, 1, :])
                        dve.tensor_copy(recs[:, q, :, 1], win2[:, q, 0, :])
                        link(dve.tensor_tensor(place[:, q, :], sli[:, 1, :], sli[:, 3, :], ALU.bitwise_or))
                        dve.tensor_copy(junk_p[:, :], sl[:, 0:1]).then_inc(placed, 1)
                    dve.sem_clear(DCH)
                    chain[0] = 0

                step(0, 0, True, False)
                step(1, 1, True, True, 0, True)
                step(2, 0, True, True, 1, True)
                step(3, 1, True, True, 2)
                with dve.Fori(2, GROUPS // 2) as i:
                    for par in range(2):
                        step(2 * i + par, par, True, True, 2 * i + par - 1)
                step(GROUPS, 0, False, True, GROUPS - 1)

        with ExitStack() as c3:
            slot_rec = sb("slot_rec", [P, 4, TPS, 2], I32, c3)
            blk_src = sb("blk_src", [P, 4, 1], I32, c3)
            src_f = sb("src_f", [P, 2, 1], FP32, c3)
            qg = sb("qg", [P, 2, HD], FP32, c3)
            qt = sb("qt", [P, TPS, H * BPT], FP32, c3)
            qd = sb("qd", [P, 2, TPS, 4, H * BPT], FP32, c3)
            valid = sb("valid", [P, TPS], FP32, c3)
            mask = sb("mask", [P, 2, TPS, BPT], FP32, c3)
            kt = sb("kt", [P, 2, BT * HD], FP32, c3)
            sc = sb("sc", [P, BT * HD], FP32, c3)
            se = sb("se", [P, BT, H, H], FP32, c3)
            ex = sb("ex", [P, BT, H, H], FP32, c3)
            mx = sb("mx", [P, BT, H], FP32, c3)
            den = sb("den", [P, BT, H], FP32, c3)
            rm = sb("rm", [P, BT, H, BPT], FP32, c3)
            at = sb("at", [P, 2, BT, H, H * BPT], FP32, c3)
            ad = sb("ad", [P, 2, BT * H, 4, H * BPT], FP32, c3)
            mt = sb("mt", [P, 2, HD], FP32, c3)
            same = sb("same", [P, 4, P], FP32, c3)
            src_b = sb("src_b", [P, 1], FP32, c3)
            early_n = sb("early_n", [P, 1], FP32, c3)
            keep = sb("keep", [P, 2], FP32, c3)
            junk3 = sb("junk3", [P, P], FP32, c3)
            row_f = sb("row_f", [P, 1], FP32, c3)
            row_i = sb("row_i", [P, 4, 1], I32, c3)
            summed = sb("summed", [P, 2, HD], FP32, c3)
            ps = c3.enter_context(nc.psum_tensor("ps", [P, 2, BT * HD], FP32))
            po = c3.enter_context(nc.psum_tensor("po", [P, 2, 512], FP32))
            prow = c3.enter_context(nc.psum_tensor("prow", [P, 512], FP32))
            psum_b = c3.enter_context(nc.psum_tensor("psum_b", [P, 512], FP32))

            rec_in = [sem(f"rec_in{i}") for i in range(4)]
            q_in = [sem("q_in0"), sem("q_in1")]
            kv_in = [sem(f"kv_in{i}") for i in range(RB)]
            added, kv_clear, late_clear = sem("added"), sem("kv_clear"), sem("late_clear")
            q_turned, q_spread, k_turned, scored = sem("q_turned"), sem("q_spread"), sem("k_turned"), sem("scored")
            shifted, exped, weighed, spread, valued = sem("shifted"), sem("exped"), sem("weighed"), sem("spread"), sem("valued")
            src_floated, src_rowed, same_built = sem("src_floated"), sem("src_rowed"), sem("same_built")
            m_turned, blocks_summed, summed_copied = sem("m_turned"), sem("blocks_summed"), sem("summed_copied")
            ADD_LAG = 6
            block = c3.enter_context(nc.Block())

            def supertiles(body, first, last, peel=4):
                for s in range(first, peel):
                    body(s, s % 4)
                return peel // 4, (NS - 1) // 4

            def rest(body, last):
                for s in range((NS - 1) // 4 * 4, last):
                    body(s, s % 4)

            def has(s, lag):
                return not isinstance(s, int) or 0 <= s - lag < NS

            def uses(s, k, ring, n):
                return n * (s // ring + 1) if isinstance(s, int) else n // ring * (s - k) + n

            @block.sync
            def _(sp):
                def load(s, k):
                    if not has(s, 0):
                        return
                    if has(s, 4):
                        sp.wait_ge(k_turned, 2 * s - 6)
                        sp.sem_inc(pass_sp, 1)
                    sp.dma_start(slot_rec[:, k, :, :].rearrange("p j f -> p (j f)"),
                                 rec[bass.ds(s * SUP, SUP), :].rearrange("(p j) f -> p (j f)", p=P)).then_inc(rec_in[k], 16)
                    view = rec[bass.ds(s * SUP, SUP), 1].rearrange("(q b o j) -> q b o j", q=4, b=BPT, o=SLOTS)[:, :, 0, :]
                    with nc.allow_non_contiguous_dma(reason="one source a block"):
                        for q in range(4):
                            sp.dma_start(blk_src[32 * q:32 * q + 32, k, :],
                                         view[q].rearrange("b j -> j b").unsqueeze(2)).then_inc(rec_in[k], 16)

                lo, hi = supertiles(load, 0, NS)
                with sp.Fori(lo, hi) as i:
                    for k in range(4):
                        load(4 * i + k, k)
                rest(load, NS)

            @block.gpsimd
            def _(gp):
                def body(s, k):
                    par = k % 2
                    if has(s, 0):
                        gp.wait_ge(rec_in[k], uses(s, k, 4, 80))
                        gp.sem_inc(pass_pool, 1)
                        if has(s, 2):
                            gp.wait_ge(q_turned, s - 1)
                            gp.sem_inc(pass_pool, 1)
                        gp.indirect_dma_start(out=qg[:, par, :], out_offset=None, in_=q_tab,
                                              in_offset=bass.IndirectOffsetOnAxis(ap=blk_src[:, k, :].bitcast(U32), axis=0),
                                              bounds_check=N - 1, oob_is_err=False).then_inc(q_in[par], 16)
                        for b in range(2):
                            r = 2 * k + b
                            if has(s, 4):
                                gp.wait_ge(valued, 2 * s + b - 7)
                                gp.sem_inc(pass_pool, 1)
                            for i in range(BT):
                                gp.indirect_dma_start(out=kv[:, r, i, :], out_offset=None, in_=kv_tab,
                                                      in_offset=bass.IndirectOffsetOnAxis(
                                                          ap=slot_rec[:, k, BT * b + i, 0:1].bitcast(U32), axis=0),
                                                      bounds_check=N - 1, oob_is_err=False).then_inc(kv_in[r], 16)
                    if has(s, ADD_LAG):
                        d = s - ADD_LAG
                        gp.wait_ge(summed_copied, d + 1)
                        gp.sem_inc(pass_pool, 1)
                        if has(d, 1):
                            gp.wait_ge(added, 16 * d)
                            gp.sem_inc(pass_pool, 1)
                        gp.indirect_dma_start(out=sums, out_offset=bass.IndirectOffsetOnAxis(
                                                  ap=row_i[:, (k - ADD_LAG) % 4, :].bitcast(U32), axis=0),
                                              in_=summed[:, (k - ADD_LAG) % 2, :], in_offset=None, bounds_check=TROWS - 1,
                                              oob_is_err=True, compute_op=ALU.add).then_inc(added, 16)

                gp.wait_ge(kv_clear, 1)
                gp.sem_inc(pass_pool, 1)
                for s in range(2):
                    body(s, s)
                gp.memset(kv[:, 4:, :, :].rearrange("p a b c -> p (a b c)"), 0.0).then_inc(late_clear, 1)
                gp.wait_ge(late_clear, 1)
                gp.sem_inc(pass_pool, 1)
                lo, hi = supertiles(body, 2, NS + ADD_LAG, 8)
                with gp.Fori(lo, hi) as i:
                    for k in range(4):
                        body(4 * i + k, k)
                rest(body, NS + ADD_LAG)
                gp.wait_ge(added, 16 * NS)

            @block.scalar
            def _(act):
                def exp(n):
                    act.wait_ge(shifted, n + 1)
                    if not isinstance(n, int) or n >= 1:
                        act.wait_ge(weighed, 2 * n)
                    act.activation(ex[:, :, :, :].rearrange("p a g h -> p (a g h)"),
                                   se[:, :, :, :].rearrange("p a g h -> p (a g h)"), ACT.Exp, scale=SCALE).then_inc(exped, 1)

                def spread_at(n, b):
                    if not isinstance(n, int) or n >= 2:
                        act.wait_ge(valued, n - 1)
                    for half in range(2):
                        act.wait_ge(weighed, 2 * n + half + 1)
                        t = slice(2 * half, 2 * half + 2)
                        for q in range(4):
                            r = slice(32 * q, 32 * q + 32)
                            last = act.activation(ad[r, b, 2 * H * half:2 * H * (half + 1), q, :],
                                                  at[r, b, t, :, :].rearrange("p i g c -> p (i g) c"), ACT.Copy)
                        last.then_inc(spread, 1)

                act.wait_ge(kv_clear, 2)

                def body(s, k):
                    par = k % 2
                    if has(s, 1):
                        spread_at(2 * s - 2, 0)
                    if has(s, -1):
                        act.wait_ge(q_turned, s + 2)
                        if has(s, 1):
                            act.wait_ge(scored, 2 * s)
                        for q in range(4):
                            r = slice(32 * q, 32 * q + 32)
                            last = act.activation(qd[r, 1 - par, :, q, :], qt[r, :, :], ACT.Copy)
                        last.then_inc(q_spread, 1)
                    if has(s, 3):
                        act.wait_ge(blocks_summed, s - 2)
                        if has(s, 5):
                            act.wait_ge(added, 16 * (s - 4))
                        act.activation(summed[:, 1 - par, :], psum_b[:, 0:HD], ACT.Copy).then_inc(summed_copied, 1)
                    if has(s, 0):
                        exp(2 * s)
                    if has(s, 1):
                        spread_at(2 * s - 1, 1)
                    if has(s, 0):
                        exp(2 * s + 1)

                lo, hi = supertiles(body, -1, NS + 3, 8)
                with act.Fori(lo, hi) as i:
                    for k in range(4):
                        body(4 * i + k, k)
                rest(body, NS + 3)

            @block.tensor
            def _(pe):
                def scores(s, par, b):
                    n = 2 * s + b
                    if b == 0:
                        pe.wait_ge(q_spread, s + 1)
                    pe.wait_ge(k_turned, n + 1)
                    if not isinstance(n, int) or n >= 2:
                        pe.wait_ge(shifted, n - 1)
                    for i in range(BT):
                        last = pe.matmul(ps[:, b, i * HD:(i + 1) * HD], qd[:, par, BT * b + i, :, :].rearrange("p q c -> p (q c)"),
                                         kt[:, b, i * HD:(i + 1) * HD], start=True, stop=True)
                    last.then_inc(scored, 1)

                def values(s, k, b):
                    n = 2 * s + b
                    if b == 0 and has(s, 2):
                        pe.wait_ge(m_turned, s - 1)
                    for half in range(2):
                        pe.wait_ge(spread, 2 * n + half + 1)
                        pe.sem_inc(pass_pe, 1)
                        for g in range(H):
                            for i in range(2 * half, 2 * half + 2):
                                last = pe.matmul(po[32 * i:32 * i + 32, k % 2, P * b:P * b + P],
                                                 kv[:, 2 * k + b, i, HD + g * DH:HD + (g + 1) * DH],
                                                 ad[:, b, H * i + g, :, :].rearrange("p q c -> p (q c)"),
                                                 start=(g == 0), stop=(g == H - 1), tile_position=(0, 32 * i))
                    last.then_inc(valued, 1)

                def body(s, k):
                    par = k % 2
                    if has(s, 0):
                        scores(s, par, 0)
                    if has(s, 3):
                        pe.wait_ge(m_turned, s - 2)
                        if has(s, 4):
                            pe.wait_ge(summed_copied, s - 3)
                        pe.matmul(psum_b[:, 0:HD], same[:, (k - 3) % 4, :], mt[:, 1 - par, :], start=True, stop=True).then_inc(blocks_summed, 1)
                    if has(s, 2):
                        values(s - 2, (k - 2) % 4, 1)
                    if has(s, 0):
                        scores(s, par, 1)
                        pe.wait_ge(src_floated, s + 1)
                        if has(s, 1):
                            pe.wait_ge(same_built, s)
                        pe.matmul(prow[:, 0:P], src_f[:, par, :].to_broadcast([P, P]), perm[:, :], start=True, stop=True)
                        pe.matmul(prow[:, P:P + 1], perm[:, :], src_f[:, par, :], start=True, stop=True).then_inc(src_rowed, 1)
                    if has(s, 1):
                        values(s - 1, (k - 1) % 4, 0)

                lo, hi = supertiles(body, 0, NS + 3)
                with pe.Fori(lo, hi) as i:
                    for k in range(4):
                        body(4 * i + k, k)
                rest(body, NS + 3)

            @block.vector
            def _(dve):
                chain = [0]

                def tick(ins):
                    chain[0] += 1
                    ins.then_inc(DCH, 1)
                    return chain[0]

                def link(ins):
                    dve.wait_ge(DCH, tick(ins))

                dve.memset(qg[:, :, :], 0.0)
                dve.memset(kv[:, 0:4, :, :].rearrange("p a b c -> p (a b c)"), 0.0).then_inc(kv_clear, 1)
                dve.memset(qd[:, :, :, :, :].rearrange("p a j q c -> p (a j q c)"), 0.0)
                dve.memset(ad[:, :, :, :, :].rearrange("p a j q c -> p (a j q c)"), 0.0).then_inc(kv_clear, 1)

                def turn_k(s, k, b):
                    r = 2 * k + b
                    n = 2 * s + b
                    dve.wait_ge(kv_in[r], uses(s, k, 4, 64))
                    if not isinstance(n, int) or n >= 2:
                        dve.wait_ge(scored, n - 1)
                    dve.transpose(kt[:, b, :].rearrange("p (i c) -> p i c", i=BT), kv[:, r, :, 0:HD]).then_inc(k_turned, 1)

                def select_and_weigh(s, par, b):
                    n = 2 * s + b
                    new = has(s, 0)
                    old = has(s, 1) if b == 0 else has(s, 0)
                    old_par = par if b == 1 else 1 - par
                    v = sc[:, :].rearrange("p (m b) -> p m b", b=BPT)
                    f = se[:, :, :, :].rearrange("p a g h -> p (a g h)")

                    def select(k):
                        if k == 0:
                            return tick(dve.tensor_scalar(f, v[:, :, 0], own[:, 0:1], None, ALU.mult))
                        return tick(dve.scalar_tensor_tensor(f, v[:, :, k], own[:, k:k + 1], f, ALU.mult, ALU.add))

                    def attention(i):
                        return dve.tensor_tensor(at[:, 1 - b, i, :, :].rearrange("p g (h b) -> p g h b", h=H),
                                                 ex[:, i, :, :].unsqueeze(3).to_broadcast([P, H, H, BPT]),
                                                 rm[:, i, :, :].unsqueeze(1).to_broadcast([P, H, H, BPT]), ALU.mult)

                    if new:
                        dve.wait_ge(scored, n + 1)
                        turned = tick(dve.transpose(sc[:, :], ps[:, b, :]))
                    if old:
                        dve.wait_ge(exped, n)
                        summed_up = tick(dve.tensor_reduce(den[:, :, :], ex[:, :, :, :].rearrange("p a g h -> p a h g"), AX.X, ALU.add))
                    if new:
                        dve.wait_ge(DCH, turned)
                        chosen = select(0)
                    if old:
                        dve.wait_ge(DCH, summed_up)
                        inverted = tick(dve.reciprocal(den[:, :, :], den[:, :, :]))
                    if new:
                        dve.wait_ge(DCH, chosen)
                        chosen = select(1)
                    if old:
                        dve.wait_ge(DCH, inverted)
                        weights = tick(dve.tensor_tensor(rm[:, :, :, :], den[:, :, :].unsqueeze(3).to_broadcast([P, BT, H, BPT]),
                                                         mask[:, old_par, BT * (1 - b):BT * (1 - b) + BT, :].unsqueeze(2)
                                                         .to_broadcast([P, BT, H, BPT]), ALU.mult))
                    if new:
                        dve.wait_ge(DCH, chosen)
                        chosen = select(2)
                    if old:
                        dve.wait_ge(DCH, weights)
                        if not isinstance(n, int) or n >= 3:
                            dve.wait_ge(spread, 2 * n - 4)
                        attention(0)
                    if new:
                        dve.wait_ge(DCH, chosen)
                        chosen = select(3)
                    if old:
                        attention(1).then_inc(weighed, 1)
                    if new:
                        dve.wait_ge(DCH, chosen)
                        most = tick(dve.tensor_reduce(mx[:, :, :], se[:, :, :, :].rearrange("p a g h -> p a h g"), AX.X, ALU.max))
                    if old:
                        attention(2)
                    if new:
                        dve.wait_ge(DCH, most)
                        dve.tensor_tensor(se[:, :, :, :], se[:, :, :, :], mx[:, :, :].unsqueeze(2).to_broadcast([P, BT, H, H]),
                                          ALU.subtract).then_inc(shifted, 1)
                    if old:
                        attention(3).then_inc(weighed, 1)

                def build_same(s, k):
                    dve.wait_ge(src_rowed, s + 1)
                    if has(s, 4):
                        dve.wait_ge(blocks_summed, s - 3)
                    link(dve.tensor_copy(src_b[:, :], prow[:, P:P + 1]))
                    dve.tensor_scalar(same[:, k, :], prow[:, 0:P], src_b[:, :], None, ALU.is_equal)
                    dve.tensor_scalar(keep[:, 1:2], src_b[:, :], float(N), None, ALU.is_lt)
                    dve.tensor_tensor(row_f[:, :], src_b[:, :], trash[:, :], ALU.subtract)
                    link(dve.scalar_tensor_tensor(junk3[:, :], prow[:, 0:P], src_b[:, :], below[:, :], ALU.is_equal,
                                                  ALU.mult, accum_out=early_n[:, :]))
                    link(dve.scalar_tensor_tensor(keep[:, 0:1], early_n[:, :], 0.0, keep[:, 1:2], ALU.is_equal, ALU.mult))
                    link(dve.scalar_tensor_tensor(row_f[:, :], row_f[:, :], keep[:, 0:1], trash[:, :], ALU.mult, ALU.add))
                    if has(s, 4):
                        dve.wait_ge(added, 16 * (s - 3))
                    dve.tensor_copy(row_i[:, k, :], row_f[:, :]).then_inc(same_built, 1)

                def body(s, k):
                    par = k % 2
                    ahead = (k + 1) % 4
                    if has(s, -1):
                        dve.wait_ge(q_in[1 - par], uses(s + 1, 1 - par, 2, 16))
                        if has(s, 0):
                            dve.wait_ge(q_spread, s + 1)
                        dve.transpose(qt[:, :, :].rearrange("p j (h b) -> p h j b", h=H),
                                      qg[:, 1 - par, :].rearrange("p (h j b) -> p h j b", h=H, j=TPS)).then_inc(q_turned, 1)
                        if has(s, 1):
                            dve.wait_ge(src_rowed, s)
                        dve.tensor_copy(src_f[:, 1 - par, :], blk_src[:, ahead, :]).then_inc(src_floated, 1)
                        valid_set = tick(dve.tensor_scalar(valid[:, :], slot_rec[:, ahead, :, 0], float(N), None, ALU.is_lt))
                    select_and_weigh(s, par, 0)
                    if has(s, -1):
                        dve.wait_ge(DCH, valid_set)
                        tick(dve.tensor_tensor(mask[:, 1 - par, :, :], valid[:, :].unsqueeze(2).to_broadcast([P, TPS, BPT]),
                                               own[:, :].unsqueeze(1).to_broadcast([P, TPS, BPT]), ALU.mult))
                        turn_k(s + 1, ahead, 0)
                    if has(s, 2):
                        dve.wait_ge(valued, 2 * s - 2)
                        if has(s, 4):
                            dve.wait_ge(blocks_summed, s - 3)
                        dve.transpose(mt[:, par, :], po[:, par, 0:HD].rearrange("p (r h b) -> p h r b", r=TPS, h=H))\
                           .then_inc(m_turned, 1)
                    select_and_weigh(s, par, 1)
                    if has(s, -1):
                        turn_k(s + 1, ahead, 1)
                    if has(s, 0):
                        build_same(s, k)
                    if chain[0]:
                        dve.wait_ge(DCH, chain[0])
                    dve.sem_clear(DCH)
                    chain[0] = 0

                lo, hi = supertiles(body, -1, NS + 2)
                with dve.Fori(lo, hi) as i:
                    for k in range(4):
                        body(4 * i + k, k)
                rest(body, NS + 2)

        with ExitStack() as c4:
            RING = 4
            xs = sb("xs", [P, NT, D], FP32, c4)
            sq = kv[:, :, :, :].rearrange("p a b c -> p (a b c)")[:, 0:NT * D].rearrange("p (t d) -> p t d", d=D)
            ms = sb("ms", [P, RING, HD], FP32, c4)
            mst = sb("mst", [P, 2, HD], FP32, c4)
            stat = sb("stat", [P, 3, NT], FP32, c4)
            pt4 = c4.enter_context(nc.psum_tensor("pt4", [P, 2, 512], FP32))
            py4 = c4.enter_context(nc.psum_tensor("py4", [P, 2, 512], FP32))
            x_all, steps, squared, rooted, y_out = sem("x_all"), sem("steps"), sem("squared"), sem("rooted"), sem("y_out")
            centred, cleared, varied = sem("centred"), sem("cleared"), sem("varied")
            ms_in = [sem(f"ms_in{i}") for i in range(RING)]
            ms_turned, mst_copied, out_done, x_added = sem("ms_turned"), sem("mst_copied"), sem("out_done"), sem("x_added")
            block = c4.enter_context(nc.Block())

            @block.sync
            def _(sp):
                def load(t, r):
                    sp.dma_start(ms[:, r, :], sums[bass.ds(t * P, P), :]).then_inc(ms_in[r], 16)

                for r in range(RING):
                    load(r, r)
                sp.wait_ge(cleared, 1)
                sp.dma_start(xs[:, 0:NT - 1, :], x[0:(NT - 1) * P, :].rearrange("(t p) d -> p t d", p=P)).then_inc(x_all, 16)
                sp.dma_start(xs[0:TAIL, NT - 1, :], x[(NT - 1) * P:N, :]).then_inc(x_all, 16)
                with sp.Fori(1, NT // RING) as i:
                    for r in range(RING):
                        sp.wait_ge(ms_turned, RING * i + r - 3)
                        sp.sem_inc(pass_sp, 1)
                        load(RING * i + r, r)
                sp.wait_ge(ms_turned, NT - RING)
                load(NT - 1, 0)
                sp.wait_ge(steps, 1)
                sp.dma_start(out[0:(NT - 1) * P, :].rearrange("(t p) d -> p t d", p=P), xs[:, 0:NT - 1, :]).then_inc(y_out, 16)
                sp.dma_start(out[(NT - 1) * P:N, :], xs[0:TAIL, NT - 1, :]).then_inc(y_out, 16)
                sp.wait_ge(y_out, 32)

            @block.tensor
            def _(pe):
                def tile(t, r, uses_r, first):
                    k = r % 2
                    pe.wait_ge(ms_in[r], 16 * uses_r)
                    for c in range(2):
                        last = pe.transpose(pt4[:, k, c * P:(c + 1) * P], ms[:, r, c * P:(c + 1) * P], ident[:, :])
                    last.then_inc(ms_turned, 1)
                    pe.wait_ge(mst_copied, t + 1)
                    if not first:
                        pe.wait_ge(x_added, t - 1)
                    for c in range(2):
                        last = pe.matmul(py4[:, k, 0:D], mst[:, k, c * P:(c + 1) * P], wot[:, c, :], start=(c == 0), stop=(c == 1))
                    last.then_inc(out_done, 1)

                for r in range(RING):
                    tile(r, r, 1, r < 2)
                with pe.Fori(1, NT // RING) as i:
                    for r in range(RING):
                        tile(RING * i + r, r, i + 1, False)
                tile(NT - 1, 0, NT // RING + 1, False)

            @block.scalar
            def _(act):
                def tile(t, k, first):
                    act.wait_ge(ms_turned, t + 1)
                    if not first:
                        act.wait_ge(out_done, t - 1)
                    act.activation(mst[:, k, :], pt4[:, k, 0:HD], ACT.Copy).then_inc(mst_copied, 1)

                tile(0, 0, True)
                tile(1, 1, True)
                with act.Fori(1, NT // 2) as i:
                    for k in range(2):
                        tile(2 * i + k, k, False)
                tile(NT - 1, 0, False)
                act.wait_ge(centred, 1)
                act.activation(sq, xs[:, :, :], ACT.Square).then_inc(squared, 1)
                act.wait_ge(varied, 1)
                act.activation(stat[:, 1, :], stat[:, 0, :], ACT.Sqrt).then_inc(rooted, 1)

            @block.vector
            def _(dve):
                chain = [0]

                def link(ins):
                    chain[0] += 1
                    ins.then_inc(DCH, 1)
                    dve.wait_ge(DCH, chain[0])

                def per_row(a):
                    return a.unsqueeze(2).to_broadcast([P, NT, D])

                dve.memset(xs[:, NT - 1, :], 0.0).then_inc(cleared, 1)
                dve.wait_ge(x_all, 32)
                for k in range(KINDS):
                    for t in range(NT):
                        last = dve.scalar_tensor_tensor(xs[:, t, :], kindw[:, k, :], counts[:, k, t:t + 1], xs[:, t, :], ALU.mult, ALU.add)
                    link(last)

                def add(t, k):
                    dve.wait_ge(out_done, t + 1)
                    dve.tensor_tensor(xs[:, bass.ds(t, 1), :].rearrange("p a d -> p (a d)"), py4[:, k, 0:D],
                                      xs[:, bass.ds(t, 1), :].rearrange("p a d -> p (a d)"), ALU.add).then_inc(x_added, 1)

                with dve.Fori(0, NT // 2) as i:
                    for k in range(2):
                        add(2 * i + k, k)
                add(NT - 1, 0)
                dve.wait_ge(x_added, NT)
                link(dve.tensor_reduce(stat[:, 2, :], xs[:, :, :], AX.X, ALU.add))
                link(dve.tensor_scalar(stat[:, 2, :], stat[:, 2, :], 1.0 / D, None, ALU.mult))
                dve.tensor_tensor(xs[:, :, :], xs[:, :, :], per_row(stat[:, 2, :]), ALU.subtract).then_inc(centred, 1)
                dve.wait_ge(squared, 1)
                link(dve.tensor_reduce(stat[:, 2, :], sq, AX.X, ALU.add))
                dve.tensor_scalar(stat[:, 0, :], stat[:, 2, :], 1.0 / D, EPS, ALU.mult, ALU.add).then_inc(varied, 1)
                dve.wait_ge(rooted, 1)
                link(dve.reciprocal(stat[:, 2, :], stat[:, 1, :]))
                dve.tensor_tensor(xs[:, :, :], xs[:, :, :], per_row(stat[:, 2, :]), ALU.mult).then_inc(steps, 1)


_INS = ["x", "src", "dst", "edge_type_3", "L0_gnn_Wq", "L0_gnn_bq", "L0_gnn_Wk", "L0_gnn_bk", "L0_gnn_Wv", "L0_gnn_bv",
        "L0_gnn_edge_emb", "L0_gnn_Wo", "L0_gnn_bo"]


def kernel(**inputs):
    import numpy as _np
    import concourse.bacc as _bacc
    from concourse import mybir as _mybir
    from concourse.bass_utils import run_bass_kernel_spmd as _run

    nc = _bacc.Bacc("TRN2", target_bir_lowering=False, num_devices=1)
    arrays, args = {}, []
    for name in _INS:
        a = _np.ascontiguousarray(inputs[name])
        arrays[f"in_{name}_dram"] = a
        args.append(nc.dram_tensor(f"in_{name}_dram", a.shape, _mybir.dt.from_np(a.dtype), kind="ExternalInput").ap())
    args.append(nc.dram_tensor("out_0_dram", (N, D), _mybir.dt.float32, kind="ExternalOutput").ap())
    build(nc, *args)
    r = _run(nc, [arrays], core_ids=[0])
    return r.results[0]["out_0_dram"]
```

```python
import numpy as np
import concourse.bass as bass
from concourse import mybir
from contextlib import ExitStack

FP32 = mybir.dt.float32
BF16 = mybir.dt.bfloat16
I32 = mybir.dt.int32
U32 = mybir.dt.uint32
ALU = mybir.AluOpType
ACT = mybir.ActivationFunctionType
AX = mybir.AxisListType

P = 128
N = 6250
E = 200000
D = 128
HD = 256
H = 8
DH = HD // H
KINDS = 3
NT = -(-N // P)
TAIL = N - (NT - 1) * P
EPS = 1e-5
SCALE = 1.0 / float(np.sqrt(np.float32(DH)))

GT = 16
GROUPS = 2 * (-(-E // (2 * GT * P)))
ET = GROUPS * GT
EFULL = E // P
HI = NT + 1
PADKEY = NT * P + P - 1
KCOLS = KINDS * NT

SLOTS = 8
BLOCKS = (E + (SLOTS - 1) * N) // SLOTS
NS = -(-BLOCKS // P)
TPS = SLOTS
SUP = P * SLOTS
BT = 4
RB = 8
BPT = 4
TROWS = N + P


def build(nc, x, src, dst, kind, wq, bq, wk, bk, wv, bv, emb, wo, bo, out):
    with ExitStack() as ctx:
        def sb(name, shape, dt=FP32, c=ctx):
            return c.enter_context(nc.sbuf_tensor(name, shape, dt))

        def sem(name):
            return ctx.enter_context(nc.semaphore(name))

        q_tab = nc.dram_tensor("q_tab", [NT * P, HD], FP32).ap()
        kv_tab = nc.dram_tensor("kv_tab", [NT * P, 2 * HD], FP32).ap()
        key_rows = nc.dram_tensor("key_rows", [ET, P], I32).ap()
        rec = nc.dram_tensor("rec", [NS * SUP, 2], I32).ap()
        sums = nc.dram_tensor("sums", [TROWS, HD], FP32).ap()

        ident = sb("ident", [P, P])
        below = sb("below", [P, P])
        above = sb("above", [P, P])
        iota_row_i = sb("iota_row_i", [P, KCOLS], I32)
        iota_row = sb("iota_row", [P, KCOLS], BF16)
        part_i = sb("part_i", [P, 1], I32)
        part_f = sb("part_f", [P, 1])
        blk_i = sb("blk_i", [P, 1], I32)
        blk_f = sb("blk_f", [P, 1])
        own = sb("own", [P, BPT])
        trash = sb("trash", [P, 1])
        wot = sb("wot", [P, 2, D])
        perm = sb("perm", [P, P])
        kindw = sb("kindw", [P, KINDS, D])
        key_c = sb("key_c", [P, ET])
        dst_c = sb("dst_c", [P, ET])
        lo_c = sb("lo_c", [P, ET])
        hi_c = sb("hi_c", [P, ET])
        cid_c = sb("cid_c", [P, ET])
        counts = sb("counts", [P, KINDS, NT])
        first_slot = sb("first_slot", [P, HI])
        kv = sb("kv", [P, RB, BT, 2 * HD])

        DCH = sem("DCH")
        pass_sp, pass_pool, pass_pe = sem("pass_sp"), sem("pass_pool"), sem("pass_pe")

        with ExitStack() as c1:
            wl = sb("wl", [P, 6, D], FP32, c1)
            wt = sb("wt", [P, 6 * P], FP32, c1)
            bias = sb("bias", [P, 3 * HD], FP32, c1)
            top = sb("top", [P, P], FP32, c1)
            wol = sb("wol", [P, HD], FP32, c1)
            bob = sb("bob", [P, D], FP32, c1)
            embt = sb("embt", [P, KINDS, 2], FP32, c1)
            xin = sb("xin", [P, 2, D], FP32, c1)
            xt = sb("xt", [P, 2, P], FP32, c1)
            qkv = sb("qkv", [P, 2, 3 * HD], FP32, c1)
            zero = sb("zero", [P, HD], FP32, c1)
            fill = kv[:, :, :, :].rearrange("p a b c -> p (a b c)")[:, 0:NS * SUP * 2 // P].bitcast(I32)
            raw = [sb(f"raw_{n}", [P, 13, P], I32, c1) for n in ("key", "dst", "kind")]
            CH = -(-ET // P)
            REM = ET - (CH - 1) * P
            FR = EFULL - (CH - 1) * P
            rawf = sb("rawf", [P, 2, P], FP32, c1)
            coli = sb("coli", [P, ET], I32, c1)
            colj = sb("colj", [P, ET], I32, c1)
            win = sb("win", [P, 2, 2, GT], FP32, c1)
            off = sb("off", [P, GT, P], BF16, c1)
            oh_lo = sb("oh_lo", [P, 2, GT, P], BF16, c1)
            oh_kh = sb("oh_kh", [P, 2, GT, KCOLS], BF16, c1)
            zero_bf = sb("zero_bf", [P, KCOLS], BF16, c1)
            total = sb("total", [P, HI], FP32, c1)
            tot_i = sb("tot_i", [P, HI], I32, c1)
            ones = sb("ones", [P, HI], FP32, c1)
            scan = sb("scan", [P, HI], FP32, c1)
            pt = c1.enter_context(nc.psum_tensor("pt", [P, 2, 512], FP32))
            pw = pt[:, :, :].rearrange("p a b -> p (a b)")
            px = c1.enter_context(nc.psum_tensor("px", [P, 512], FP32))
            pq = c1.enter_context(nc.psum_tensor("pq", [P, 2, 2, 512], FP32))
            hist = c1.enter_context(nc.psum_tensor("hist", [P, 512], FP32))
            HALF = 3 * HD // 2
            ACT_TILES = 7
            assert GROUPS == 2 * NT

            weights_in, emb_in, bias_in = sem("weights_in"), sem("emb_in"), sem("bias_in")
            consts, wt_done, wo_done, wo_copied = sem("consts"), sem("wt_done"), sem("wo_done"), sem("wo_copied")
            wt_copied, kindw_done, pads_set = sem("wt_copied"), sem("kindw_done"), sem("pads_set")
            x_in = [sem("x_in0"), sem("x_in1")]
            x_turned, xt_copied, qkv_done, qkv_copied = sem("x_turned"), sem("xt_copied"), sem("qkv_done"), sem("qkv_copied")
            qkv_out = [sem("qkv_out0"), sem("qkv_out1")]
            inits_out, fill_set = sem("inits_out"), sem("fill_set")
            pads1, edges_in, rows_out = sem("pads1"), sem("edges_in"), sem("rows_out")
            raw_f, turned, cols_done = sem("raw_f"), sem("turned"), sem("cols_done")
            windows, apart, act_onehots = sem("windows"), sem("apart"), sem("act_onehots")
            onehots, counted, row_tot, prefixed = sem("onehots"), sem("counted"), sem("row_tot"), sem("prefixed")
            block = c1.enter_context(nc.Block())

            @block.sync
            def _(sp):
                for i, w in enumerate((wq, wk, wv)):
                    sp.dma_start(wl[:, 2 * i:2 * i + 2, :], w.rearrange("(c p) f -> p c f", p=P)).then_inc(weights_in, 16)
                sp.dma_start(wol[:, :], wo).then_inc(weights_in, 16)
                sp.dma_start(bob[:, :], bo.unsqueeze(0).to_broadcast([P, D])).then_inc(bias_in, 16)
                sp.wait_ge(pads1, 3)
                for r, a in zip(raw, (src, dst, kind)):
                    sp.dma_start(r[:, 0:CH - 1, :], a[0:(CH - 1) * P * P].rearrange("(c q e) -> q c e", q=P, e=P)).then_inc(edges_in, 16)
                    sp.dma_start(r[0:FR, CH - 1, :], a[(CH - 1) * P * P:EFULL * P].rearrange("(q e) -> q e", e=P)).then_inc(edges_in, 16)
                    sp.dma_start(r[FR:FR + 1, CH - 1, 0:E - EFULL * P], a[EFULL * P:E].unsqueeze(0)).then_inc(edges_in, 16)
                for i, b in enumerate((bq, bk, bv)):
                    sp.dma_start(bias[:, i * HD:(i + 1) * HD], b.unsqueeze(0).to_broadcast([P, HD])).then_inc(bias_in, 16)

                def load_x(t, par, rows):
                    sp.dma_start(xin[0:rows, par, :], x[bass.ds(t * P, rows), :]).then_inc(x_in[par], 16)

                def store_qkv(t, par):
                    sp.wait_ge(qkv_copied, t + 1)
                    sp.sem_inc(pass_sp, 1)
                    sp.dma_start(q_tab[bass.ds(t * P, P), :], qkv[:, par, 0:HD]).then_inc(qkv_out[par], 16)
                    sp.dma_start(kv_tab[bass.ds(t * P, P), :], qkv[:, par, HD:]).then_inc(qkv_out[par], 16)

                sp.wait_ge(pads_set, 1)
                load_x(0, 0, P)
                load_x(1, 1, P)
                sp.wait_ge(edges_in, 16 * 9)
                sp.dma_start(key_rows[0:(CH - 1) * P, :].rearrange("(c q) e -> q c e", q=P), raw[0][:, 0:CH - 1, :]).then_inc(rows_out, 16)
                sp.dma_start(key_rows[(CH - 1) * P:ET, :], raw[0][0:REM, CH - 1, :]).then_inc(rows_out, 16)

                def tile(t, par, rows=P):
                    sp.wait_ge(x_turned, t - 1)
                    sp.sem_inc(pass_sp, 1)
                    load_x(t, par, rows)
                    if not isinstance(t, int) or t >= 4:
                        store_qkv(t - 4, par)

                for t in range(2, 4):
                    tile(t, t % 2)
                with sp.Fori(2, NT // 2) as i:
                    for par in range(2):
                        tile(2 * i + par, par)
                tile(NT - 1, 0, TAIL)
                for t in range(NT - 4, NT):
                    store_qkv(t, t % 2)
                sp.wait_ge(qkv_out[0], 32 * (NT // 2 + 1))
                sp.wait_ge(qkv_out[1], 32 * (NT // 2))
                sp.wait_ge(rows_out, 32)

            @block.gpsimd
            def _(gp):
                gp.memset(ident[:, :], 0.0).then_inc(pads_gp := sem("pads_gp"), 1)
                gp.memset(below[:, :], 1.0).then_inc(pads_gp, 1)
                gp.memset(above[:, :], 1.0).then_inc(pads_gp, 1)
                gp.iota(part_i[:, :], pattern=[[0, 1]], base=0, channel_multiplier=1).then_inc(consts, 1)
                gp.iota(iota_row_i[:, :], pattern=[[1, KCOLS]], base=0, channel_multiplier=0).then_inc(consts, 1)
                gp.wait_ge(pads_gp, 3)
                gp.affine_select(out=ident[:, :], in_=ident[:, :], compare_op=ALU.not_equal, fill=1.0,
                                 base=0, pattern=[[-1, P]], channel_multiplier=1).then_inc(consts, 1)
                gp.affine_select(out=below[:, :], in_=below[:, :], compare_op=ALU.is_gt, fill=0.0,
                                 base=0, pattern=[[-1, P]], channel_multiplier=1).then_inc(consts, 1)
                gp.affine_select(out=above[:, :], in_=above[:, :], compare_op=ALU.is_gt, fill=0.0,
                                 base=0, pattern=[[1, P]], channel_multiplier=-1).then_inc(consts, 1)
                with nc.allow_non_contiguous_dma(reason="768 elements, once"):
                    for k in range(KINDS):
                        gp.dma_start(embt[:, k, :], emb[k, :].rearrange("(c p) -> p c", p=P)).then_inc(emb_in, 16)

            @block.scalar
            def _(act):
                act.wait_ge(edges_in, 16 * 9)
                act.wait_ge(fill_set, 1)
                act.dma_start(rec.rearrange("(p s) f -> p (s f)", p=P), fill).then_inc(inits_out, 16)
                act.wait_ge(fill_set, 2)
                nfull = TROWS // P
                act.dma_start(sums[0:nfull * P, :].rearrange("(t p) d -> p t d", p=P),
                              zero[:, :].unsqueeze(1).to_broadcast([P, nfull, HD])).then_inc(inits_out, 16)
                act.dma_start(sums[nfull * P:TROWS, :], zero[0:TROWS - nfull * P, :]).then_inc(inits_out, 16)

                def copy_qkv(t, par):
                    act.wait_ge(qkv_done, t + 1)
                    if not isinstance(t, int) or t >= 2:
                        act.wait_ge(qkv_out[par], 32 * (t // 2) if isinstance(t, int) else 16 * (t - par))
                    act.activation(qkv[:, par, :].rearrange("p (c n) -> p c n", c=2), pq[:, par, :, 0:HALF], ACT.Copy)\
                       .then_inc(qkv_copied, 1)

                def onehot(g, par):
                    act.wait_ge(windows, g + 1)

                    def match(k):
                        act.wait_ge(apart, g * ACT_TILES + k + 1)
                        return act.activation(oh_lo[:, par, k, :], off[:, k, :], ACT.Relu, scale=-1.0, bias=1.0)

                    for k in range(ACT_TILES):
                        act.activation(off[:, k, :], iota_row[:, 0:P], ACT.Square, scale=-1.0,
                                       bias=win[:, par, 0, k:k + 1]).then_inc(apart, 1)
                        if k:
                            match(k - 1)
                    match(ACT_TILES - 1).then_inc(act_onehots, 1)

                def tile(t, par):
                    for j in range(2):
                        onehot(2 * t + j, j)
                    act.wait_ge(x_turned, t + 1)
                    if not isinstance(t, int) or t >= 2:
                        act.wait_ge(qkv_done, t - 1)
                    act.activation(xt[:, par, :], px[:, 0:P], ACT.Copy).then_inc(xt_copied, 1)
                    if not isinstance(t, int) or t >= 2:
                        copy_qkv(t - 2, par)

                for t in range(4):
                    tile(t, t % 2)
                with act.Fori(2, NT // 2) as i:
                    for par in range(2):
                        tile(2 * i + par, par)
                tile(NT - 1, 0)
                copy_qkv(NT - 2, 1)
                copy_qkv(NT - 1, 0)
                act.wait_ge(inits_out, 48)

            @block.tensor
            def _(pe):
                pe.wait_ge(consts, 5)
                pe.wait_ge(weights_in, 64)
                for c in range(6):
                    last = pe.transpose(pw[:, c * P:(c + 1) * P], wl[:, c, :], ident[:, :])
                last.then_inc(wt_done, 1)
                pe.wait_ge(wt_copied, 1)
                for c in range(2):
                    last = pe.transpose(pw[:, c * P:(c + 1) * P], wol[:, c * P:(c + 1) * P], ident[:, :])
                last.then_inc(wo_done, 1)
                pe.wait_ge(wo_copied, 1)
                pe.wait_ge(emb_in, 16 * KINDS)
                for k in range(KINDS):
                    for c in range(2):
                        last = pe.matmul(pw[:, k * D:(k + 1) * D], embt[:, k, c:c + 1].to_broadcast([P, P]),
                                         wot[:, c, :], start=(c == 0), stop=(c == 1))
                last.then_inc(kindw_done, 1)

                n = 0
                for a in range(3):
                    for c in range(CH):
                        m = P if c < CH - 1 else REM
                        pe.wait_ge(raw_f, n + 1)
                        if n >= 2:
                            pe.wait_ge(cols_done, n - 1)
                        pe.transpose(pt[:, n % 2, 0:m], rawf[0:m, n % 2, :], ident[0:m, 0:m]).then_inc(turned, 1)
                        n += 1
                pe.wait_ge(onehots, 1)
                pe.matmul(hist[:, 0:KCOLS], zero_bf[:, 0:P], zero_bf[:, :], start=True, stop=False, skip_group_check=True)
                pe.wait_ge(bias_in, 64)

                def count(g, par):
                    pe.wait_ge(onehots, g + 1)
                    pe.wait_ge(act_onehots, g + 1)
                    for k in range(GT):
                        last = pe.matmul(hist[:, 0:KCOLS], oh_lo[:, par, k, :], oh_kh[:, par, k, :],
                                         start=False, stop=False, skip_group_check=True)
                    last.then_inc(counted, 1)

                def project(t, par):
                    pe.wait_ge(xt_copied, t + 1)
                    if not isinstance(t, int) or t >= 2:
                        pe.wait_ge(qkv_copied, t - 1)
                    for c in range(2):
                        cols = slice(c * HALF, (c + 1) * HALF)
                        pe.matmul(pq[:, par, c, 0:HALF], top[:, :], bias[:, cols], start=True, stop=False)
                        last = pe.matmul(pq[:, par, c, 0:HALF], xt[:, par, :], wt[:, cols], start=False, stop=True)
                    last.then_inc(qkv_done, 1)

                def tile(t, par):
                    pe.wait_ge(x_in[par], 16 * (t // 2 + 1) if isinstance(t, int) else 8 * (t - par) + 16)
                    if not isinstance(t, int) or t >= 1:
                        pe.wait_ge(xt_copied, t)
                    pe.transpose(px[:, 0:P], xin[:, par, :], ident[:, :]).then_inc(x_turned, 1)
                    for j in range(2):
                        count(2 * t + j, j)
                    if not isinstance(t, int) or t >= 1:
                        project(t - 1, 1 - par)

                for t in range(4):
                    tile(t, t % 2)
                with pe.Fori(2, NT // 2) as i:
                    for par in range(2):
                        tile(2 * i + par, par)
                tile(NT - 1, 0)
                project(NT - 1, 0)
                pe.wait_ge(row_tot, 1)
                pe.matmul(pt[:, 0, 0:1], above[:, :], scan[:, NT - 1:NT], start=True, stop=True).then_inc(prefixed, 1)

            @block.vector
            def _(dve):
                chain = [0]

                def link(ins):
                    chain[0] += 1
                    ins.then_inc(DCH, 1)
                    dve.wait_ge(DCH, chain[0])

                for r, pad in zip(raw, (PADKEY, PADKEY, KINDS)):
                    dve.memset(r[:, CH - 1, :], pad).then_inc(pads1, 1)
                dve.memset(xin[:, :, :], 0.0).then_inc(pads_set, 1)
                link(dve.memset(top[:, :], 0.0))
                dve.memset(top[0:1, :], 1.0)
                dve.memset(fill, PADKEY).then_inc(fill_set, 1)
                dve.memset(zero[:, :], 0.0).then_inc(fill_set, 1)
                dve.memset(zero_bf[:, :], 0.0)
                dve.memset(ones[:, :], 1.0)
                dve.wait_ge(consts, 5)
                link(dve.tensor_copy(iota_row[:, :], iota_row_i[:, :]))
                link(dve.tensor_copy(part_f[:, :], part_i[:, :]))
                link(dve.tensor_scalar(blk_i[:, :], part_i[:, :], 3, 3, ALU.logical_shift_right, ALU.bitwise_and))
                link(dve.tensor_copy(blk_f[:, :], blk_i[:, :]))
                link(dve.tensor_scalar(own[:, :], iota_row[:, 0:BPT], blk_f[:, 0:1], None, ALU.is_equal))
                link(dve.tensor_scalar(trash[:, :], part_f[:, :], float(N), None, ALU.add))
                dve.wait_ge(wt_done, 1)
                dve.tensor_copy(wt[:, :], pw[:, 0:6 * P]).then_inc(wt_copied, 1)
                for i in range(BT):
                    last = dve.tensor_copy(perm[:, 32 * i:32 * i + 32].rearrange("p (b q k) -> p b q k", b=2, q=4),
                                           ident[:, :].rearrange("p (q b i k) -> p i b q k", q=4, b=2, i=BT)[:, i])
                link(last)
                dve.wait_ge(wo_done, 1)
                dve.tensor_copy(wot[:, :, :].rearrange("p c d -> p (c d)"), pw[:, 0:2 * D]).then_inc(wo_copied, 1)
                dve.wait_ge(kindw_done, 1)
                dve.wait_ge(bias_in, 64)
                for k in range(KINDS):
                    link(dve.tensor_tensor(kindw[:, k, :], pw[:, k * D:(k + 1) * D], bob[:, :], ALU.add))
                dve.sem_clear(DCH)
                chain[0] = 0
                dve.wait_ge(edges_in, 16 * 9)
                blocks = [(a, c) for a in range(3) for c in range(CH)]

                def to_float(n):
                    a, c = blocks[n]
                    if n >= 2:
                        dve.wait_ge(turned, n - 1)
                    m = P if c < CH - 1 else REM
                    dve.tensor_copy(rawf[0:m, n % 2, :], raw[a][0:m, c, :]).then_inc(raw_f, 1)

                to_float(0)
                for n, (a, c) in enumerate(blocks):
                    if n + 1 < len(blocks):
                        to_float(n + 1)
                    m = P if c < CH - 1 else REM
                    dve.wait_ge(turned, n + 1)
                    dve.tensor_copy((key_c, dst_c, cid_c)[a][:, c * P:c * P + m], pt[:, n % 2, 0:m]).then_inc(cols_done, 1)
                dve.wait_ge(cols_done, len(blocks))
                link(dve.tensor_copy(coli[:, :], key_c[:, :]))
                link(dve.tensor_scalar(colj[:, :], coli[:, :], P - 1, None, ALU.bitwise_and))
                link(dve.tensor_copy(lo_c[:, :], colj[:, :]))
                link(dve.tensor_scalar(colj[:, :], coli[:, :], 7, None, ALU.logical_shift_right))
                link(dve.tensor_copy(hi_c[:, :], colj[:, :]))
                link(dve.scalar_tensor_tensor(cid_c[:, :], cid_c[:, :], float(NT), hi_c[:, :], ALU.mult, ALU.add))
                dve.sem_clear(DCH)

                def onehot(g, par, first):
                    if not first:
                        dve.wait_ge(counted, g - 1)
                    dve.tensor_copy(win[:, par, 0, :], lo_c[:, bass.ds(g * GT, GT)]).then_inc(windows, 1)
                    dve.tensor_copy(win[:, par, 1, :], cid_c[:, bass.ds(g * GT, GT)]).then_inc(DCH, 1)
                    dve.wait_ge(DCH, par + 1)
                    for k in range(GT):
                        if k >= ACT_TILES:
                            dve.tensor_scalar(oh_lo[:, par, k, :], iota_row[:, 0:P], win[:, par, 0, k:k + 1], None, ALU.is_equal)
                        last = dve.tensor_scalar(oh_kh[:, par, k, :], iota_row[:, :], win[:, par, 1, k:k + 1], None, ALU.is_equal)
                    last.then_inc(onehots, 1)

                onehot(0, 0, True)
                onehot(1, 1, True)
                dve.sem_clear(DCH)
                with dve.Fori(1, GROUPS // 2) as i:
                    for par in range(2):
                        onehot(2 * i + par, par, False)
                    dve.sem_clear(DCH)
                dve.wait_ge(counted, GROUPS)
                chain[0] = 0
                link(dve.tensor_copy(counts[:, :, :].rearrange("p k h -> p (k h)"), hist[:, 0:KCOLS]))
                link(dve.memset(total[:, :], 0.0))
                link(dve.tensor_tensor(total[:, 0:NT], counts[:, 0, :], counts[:, 1, :], ALU.add))
                link(dve.tensor_tensor(total[:, 0:NT], total[:, 0:NT], counts[:, 2, :], ALU.add))
                link(dve.tensor_scalar(total[:, 0:NT], total[:, 0:NT], float(SLOTS - 1), None, ALU.add))
                link(dve.tensor_copy(tot_i[:, :], total[:, :]))
                link(dve.tensor_scalar(tot_i[:, :], tot_i[:, :], 3, 3, ALU.logical_shift_right, ALU.logical_shift_left))
                link(dve.tensor_copy(total[:, :], tot_i[:, :]))
                link(dve.tensor_tensor_scan(scan[:, :], ones[:, :], total[:, :], 0.0, ALU.mult, ALU.add))
                dve.tensor_copy(part_f[:, :], part_i[:, :]).then_inc(row_tot, 1)
                link(dve.tensor_tensor(total[:, :], scan[:, :], total[:, :], ALU.subtract))
                dve.wait_ge(prefixed, 1)
                link(dve.tensor_scalar(first_slot[:, :], total[:, :], pt[:, 0, 0:1], None, ALU.add))
                dve.sem_clear(DCH)

        with ExitStack() as c2:
            krow = sb("krow", [P, 2, GT * P], I32, c2)
            lrow = sb("lrow", [P, 2, GT * P], I32, c2)
            neg_part = sb("neg_part", [P, 1], FP32, c2)
            far = sb("far", [P, 4, P], FP32, c2)
            win2 = sb("win2", [P, 2, 4, GT], FP32, c2)
            oh_e = sb("oh_e", [P, 2, GT, P], BF16, c2)
            oh_h = sb("oh_h", [P, 2, GT, HI], BF16, c2)
            oh_t = sb("oh_t", [P, 2, GT, P], FP32, c2)
            taken = sb("taken", [P, 2, HI], FP32, c2)
            junk = sb("junk", [P, GT, P], BF16, c2)
            junk_s = sb("junk_s", [P, GT, HI], FP32, c2)
            junk_p = sb("junk_p", [P, 1], FP32, c2)
            within = sb("within", [P, 2, GT], FP32, c2)
            base = sb("base", [P, 2, GT], FP32, c2)
            sl = sb("sl", [P, GT], FP32, c2)
            sli = sb("sli", [P, 4, GT], I32, c2)
            recs = sb("recs", [P, 2, GT, 2], I32, c2)
            place = sb("place", [P, 2, GT], I32, c2)
            free_slot = c2.enter_context(nc.psum_tensor("free_slot", [P, 512], FP32))
            look = c2.enter_context(nc.psum_tensor("look", [P, 4, 512], FP32))

            krow_in = [sem("krow_in0"), sem("krow_in1")]
            krow_read, ohs, tallied, snapped = sem("krow_read"), sem("ohs"), sem("tallied"), sem("snapped")
            looked, selected, placed = sem("looked"), sem("selected"), sem("placed")
            lows, distant, turned_t = sem("lows"), sem("distant"), sem("turned_t")
            scattered = [sem("scattered0"), sem("scattered1")]
            block = c2.enter_context(nc.Block())

            @block.sync
            def _(sp):
                def load(g, par, first):
                    if not first:
                        sp.wait_ge(krow_read, g - 1)
                        sp.sem_inc(pass_sp, 1)
                    sp.dma_start(krow[:, par, :], key_rows[bass.ds(g * GT, GT), :].rearrange("t e -> (t e)")
                                 .unsqueeze(0).to_broadcast([P, GT * P])).then_inc(krow_in[par], 16)

                load(0, 0, True)
                load(1, 1, True)
                with sp.Fori(1, GROUPS // 2) as i:
                    for par in range(2):
                        load(2 * i + par, par, False)

            @block.gpsimd
            def _(gp):
                def scatter(g, par):
                    gp.wait_ge(placed, g + 1)
                    gp.sem_inc(pass_pool, 1)
                    for k in range(GT):
                        gp.indirect_dma_start(out=rec, out_offset=bass.IndirectOffsetOnAxis(ap=place[:, par, k:k + 1].bitcast(U32), axis=0),
                                              in_=recs[:, par, k, :], in_offset=None, bounds_check=NS * SUP - 1,
                                              oob_is_err=False).then_inc(scattered[par], 16)

                with gp.Fori(0, GROUPS // 2) as i:
                    for par in range(2):
                        scatter(2 * i + par, par)
                for par in range(2):
                    gp.wait_ge(scattered[par], 16 * ET // 2)

            @block.scalar
            def _(act):
                def snap(t, k, first):
                    act.wait_ge(tallied, t + 1)
                    if not first:
                        act.wait_ge(looked, t - 1)
                    act.activation(taken[:, k % 2, :], free_slot[:, 0:HI], ACT.Copy).then_inc(snapped, 1)

                def distance(g, t, par, k):
                    if k == 0:
                        act.wait_ge(lows, g + 1)
                    act.activation(far[:, k % 4, :], lrow[:, par, k * P:(k + 1) * P], ACT.Square,
                                   bias=neg_part[:, 0:1]).then_inc(distant, 1)

                def match(t, par, k, first):
                    act.wait_ge(distant, t + 1)
                    if not first:
                        act.wait_ge(looked, t - 2 * GT + 1)
                    act.activation(oh_t[:, par, k, :], far[:, k % 4, :], ACT.Relu, scale=-1.0, bias=1.0).then_inc(turned_t, 1)

                def tile(g, t, k, par, first, snaps, last):
                    if snaps:
                        snap(t - GT, k, first)
                    if not last:
                        distance(g + 1, t, 1 - par, k)
                        if k:
                            match(t - 1, 1 - par, k - 1, isinstance(t, int) and t - 1 < 2 * GT)
                        if k == GT - 1:
                            match(t, 1 - par, k, isinstance(t, int) and t < 2 * GT)

                for g in range(-1, 2):
                    for k in range(GT):
                        tile(g, (g + 1) * GT + k, k, g % 2, g == 0 and k < 2, g >= 0, False)
                with act.Fori(1, GROUPS // 2 - 1) as i:
                    for par in range(2):
                        for k in range(GT):
                            tile(2 * i + par, 2 * GT * i + (par + 1) * GT + k, k, par, False, True, False)
                for g in range(GROUPS - 2, GROUPS):
                    for k in range(GT):
                        tile(g, (g + 1) * GT + k, k, g % 2, False, True, g == GROUPS - 1)

            @block.tensor
            def _(pe):
                pe.matmul(free_slot[:, 0:HI], ident[:, :], first_slot[:, :], start=True, stop=False,
                          skip_group_check=True).then_inc(tallied, 1)

                def tile(g, t, par, k, first):
                    if k == 0:
                        pe.wait_ge(ohs, g + 1)
                    pe.wait_ge(snapped, t + 1)
                    pe.matmul(free_slot[:, 0:HI], oh_e[:, par, k, :], oh_h[:, par, k, :], start=False, stop=False,
                              skip_group_check=True).then_inc(tallied, 1)
                    if not first:
                        pe.wait_ge(selected, t - 3)
                    pe.wait_ge(turned_t, t + 1)
                    pe.matmul(look[:, k % 4, 0:HI], oh_t[:, par, k, :], taken[:, k % 2, :], start=True,
                              stop=True).then_inc(looked, 1)

                for k in range(2 * GT):
                    tile(k // GT, k, k // GT, k % GT, k < 4)
                with pe.Fori(1, GROUPS // 2) as i:
                    for k in range(2 * GT):
                        tile(2 * i + k // GT, 2 * GT * i + k, k // GT, k % GT, False)

            @block.vector
            def _(dve):
                chain = [0]

                def link(ins):
                    chain[0] += 1
                    ins.then_inc(DCH, 1)
                    dve.wait_ge(DCH, chain[0])

                def step(g, par, do_oh, do_sel, gs=None, early=False):
                    q = 1 - par
                    if do_oh:
                        for n, a in enumerate((key_c, dst_c, lo_c, hi_c)):
                            last = dve.tensor_copy(win2[:, par, n, :], a[:, bass.ds(g * GT, GT)])
                        link(last)
                        dve.wait_ge(krow_in[par], 16 * (g // 2 + 1) if isinstance(g, int) else 8 * (g - par) + 16)
                        if not isinstance(g, int) or g >= 2:
                            dve.wait_ge(distant, (g - 1) * GT)
                        dve.tensor_scalar(lrow[:, par, :], krow[:, par, :], P - 1, None, ALU.bitwise_and).then_inc(lows, 1)
                    for k in range(GT):
                        if do_oh:
                            dve.tensor_scalar(oh_e[:, par, k, :], iota_row[:, 0:P], win2[:, par, 2, k:k + 1], None, ALU.is_equal)
                            last = dve.tensor_scalar(oh_h[:, par, k, :], iota_row[:, 0:HI], win2[:, par, 3, k:k + 1], None, ALU.is_equal)
                            if k == GT - 1:
                                last.then_inc(ohs, 1)
                            last = dve.scalar_tensor_tensor(junk[:, k, :], krow[:, par, k * P:(k + 1) * P], win2[:, par, 0, k:k + 1],
                                                            below[:, :], ALU.is_equal, ALU.mult, accum_out=within[:, par, k:k + 1])
                            if k == GT - 1:
                                last.then_inc(krow_read, 1)
                        if do_sel:
                            dve.wait_ge(looked, gs * GT + k + 1)
                            last = dve.scalar_tensor_tensor(junk_s[:, k, :], iota_row[:, 0:HI], win2[:, q, 3, k:k + 1],
                                                            look[:, k % 4, 0:HI], ALU.is_equal, ALU.mult,
                                                            accum_out=base[:, q, k:k + 1])
                            last.then_inc(selected, 1)
                    if do_sel:
                        dve.wait_ge(selected, gs * GT + GT)
                        link(dve.tensor_tensor(sl[:, :], base[:, q, :], within[:, q, :], ALU.add))
                        if not early:
                            dve.wait_ge(scattered[q], (GT * 16) * (gs // 2) if isinstance(gs, int) else (GT * 8) * (gs - q))
                        link(dve.tensor_copy(sli[:, 0, :], sl[:, :]))
                        link(dve.tensor_scalar(sli[:, 1, :], sli[:, 0, :], 31, 3, ALU.bitwise_and, ALU.logical_shift_left))
                        link(dve.tensor_scalar(sli[:, 2, :], sli[:, 0, :], 5, 7, ALU.logical_shift_right, ALU.bitwise_and))
                        link(dve.tensor_scalar(sli[:, 3, :], sli[:, 0, :], 8, 8, ALU.logical_shift_right, ALU.logical_shift_left))
                        link(dve.tensor_tensor(sli[:, 1, :], sli[:, 1, :], sli[:, 2, :], ALU.bitwise_or))
                        dve.tensor_copy(recs[:, q, :, 0], win2[:, q, 1, :])
                        dve.tensor_copy(recs[:, q, :, 1], win2[:, q, 0, :])
                        link(dve.tensor_tensor(place[:, q, :], sli[:, 1, :], sli[:, 3, :], ALU.bitwise_or))
                        dve.tensor_copy(junk_p[:, :], sl[:, 0:1]).then_inc(placed, 1)
                    dve.sem_clear(DCH)
                    chain[0] = 0

                link(dve.tensor_scalar(neg_part[:, :], part_f[:, :], -1.0, None, ALU.mult))
                step(0, 0, True, False)
                step(1, 1, True, True, 0, True)
                step(2, 0, True, True, 1, True)
                step(3, 1, True, True, 2)
                with dve.Fori(2, GROUPS // 2) as i:
                    for par in range(2):
                        step(2 * i + par, par, True, True, 2 * i + par - 1)
                step(GROUPS, 0, False, True, GROUPS - 1)

        with ExitStack() as c3:
            slot_rec = sb("slot_rec", [P, 4, TPS, 2], I32, c3)
            blk_src = sb("blk_src", [P, 4, 1], I32, c3)
            src_f = sb("src_f", [P, 2, 1], FP32, c3)
            qg = sb("qg", [P, 2, HD], FP32, c3)
            qt = sb("qt", [P, TPS, H * BPT], FP32, c3)
            qd = sb("qd", [P, 2, TPS, 4, H * BPT], FP32, c3)
            valid = sb("valid", [P, TPS], FP32, c3)
            mask = sb("mask", [P, 2, TPS, BPT], FP32, c3)
            kt = sb("kt", [P, 2, BT * HD], FP32, c3)
            group_i = sb("group_i", [P, 2], I32, c3)
            group_f = sb("group_f", [P, 2], FP32, c3)
            take = sb("take", [P, BPT], FP32, c3)
            take_s = sb("take_s", [P, BPT, SLOTS], FP32, c3)
            gather_h = sb("gather_h", [P, BT, P], FP32, c3)
            own_sc = sb("own_sc", [P, 2, BT * HD], FP32, c3)
            se = sb("se", [P, 2, H, BT * H], FP32, c3)
            ex = sb("ex", [P, 2, H, BT * H], FP32, c3)
            mx = sb("mx", [P, BT * H], FP32, c3)
            den = sb("den", [P, BT * H], FP32, c3)
            rm = sb("rm", [P, BT, H, BPT], FP32, c3)
            at = sb("at", [P, 2, BT, H, H * BPT], FP32, c3)
            ad = sb("ad", [P, 2, BT * H, 4, H * BPT], FP32, c3)
            mt = sb("mt", [P, 2, HD], FP32, c3)
            same = sb("same", [P, 4, P], FP32, c3)
            src_b = sb("src_b", [P, 1], FP32, c3)
            early_n = sb("early_n", [P, 1], FP32, c3)
            keep = sb("keep", [P, 2], FP32, c3)
            junk3 = sb("junk3", [P, P], FP32, c3)
            row_f = sb("row_f", [P, 1], FP32, c3)
            row_i = sb("row_i", [P, 4, 1], I32, c3)
            summed = sb("summed", [P, 2, HD], FP32, c3)
            ps = c3.enter_context(nc.psum_tensor("ps", [P, 2, BT * HD], FP32))
            po = c3.enter_context(nc.psum_tensor("po", [P, 2, 512], FP32))
            pt = c3.enter_context(nc.psum_tensor("pgat", [P, 512], FP32))
            pmix = c3.enter_context(nc.psum_tensor("pmix", [P, 512], FP32))
            psum_b = pmix[:, 0:HD]
            prow, pcol = pmix[:, HD:HD + P], pmix[:, HD + P:HD + P + 1]

            rec_in = [sem(f"rec_in{i}") for i in range(4)]
            q_in = [sem("q_in0"), sem("q_in1")]
            kv_in = [sem(f"kv_in{i}") for i in range(RB)]
            added, kv_clear, late_clear = sem("added"), sem("kv_clear"), sem("late_clear")
            q_turned, q_spread, k_turned, scored = sem("q_turned"), sem("q_spread"), sem("k_turned"), sem("scored")
            shifted, exped, weighed, spread, valued = sem("shifted"), sem("exped"), sem("weighed"), sem("spread"), sem("valued")
            src_floated, src_rowed, same_built = sem("src_floated"), sem("src_rowed"), sem("same_built")
            m_turned, blocks_summed, summed_copied = sem("m_turned"), sem("blocks_summed"), sem("summed_copied")
            picked_act, picked_dve, gathered, t_turned = sem("picked_act"), sem("picked_dve"), sem("gathered"), sem("t_turned")
            ADD_LAG = 6
            block = c3.enter_context(nc.Block())

            PEEL = 8
            LOOPS = (PEEL // 4, (NS - 2) // 4)
            TAIL_S = LOOPS[1] * 4


            def has(s, lag):
                return not isinstance(s, int) or 0 <= s - lag < NS

            def uses(s, k, ring, n):
                return n * (s // ring + 1) if isinstance(s, int) else n // ring * (s - k) + n

            @block.sync
            def _(sp):
                def load(s, k):
                    if not has(s, 0):
                        return
                    if has(s, 4):
                        sp.wait_ge(k_turned, 2 * s - 6)
                        sp.sem_inc(pass_sp, 1)
                    sp.dma_start(slot_rec[:, k, :, :].rearrange("p j f -> p (j f)"),
                                 rec[bass.ds(s * SUP, SUP), :].rearrange("(p j) f -> p (j f)", p=P)).then_inc(rec_in[k], 16)
                    view = rec[bass.ds(s * SUP, SUP), 1].rearrange("(q b o j) -> q b o j", q=4, b=BPT, o=SLOTS)[:, :, 0, :]
                    with nc.allow_non_contiguous_dma(reason="one source a block"):
                        for q in range(4):
                            sp.dma_start(blk_src[32 * q:32 * q + 32, k, :],
                                         view[q].rearrange("b j -> j b").unsqueeze(2)).then_inc(rec_in[k], 16)

                for s in range(PEEL):
                    load(s, s % 4)
                with sp.Fori(*LOOPS) as i:
                    for k in range(4):
                        load(4 * i + k, k)
                for s in range(TAIL_S, NS):
                    load(s, s % 4)

            @block.gpsimd
            def _(gp):
                def body(s, k):
                    par = k % 2
                    if has(s, 0):
                        gp.wait_ge(rec_in[k], uses(s, k, 4, 80))
                        gp.sem_inc(pass_pool, 1)
                        if has(s, 2):
                            gp.wait_ge(q_turned, s - 1)
                            gp.sem_inc(pass_pool, 1)
                        gp.indirect_dma_start(out=qg[:, par, :], out_offset=None, in_=q_tab,
                                              in_offset=bass.IndirectOffsetOnAxis(ap=blk_src[:, k, :].bitcast(U32), axis=0),
                                              bounds_check=N - 1, oob_is_err=False).then_inc(q_in[par], 16)
                        for b in range(2):
                            r = 2 * k + b
                            if has(s, 4):
                                gp.wait_ge(valued, 2 * s + b - 7)
                                gp.sem_inc(pass_pool, 1)
                            for i in range(BT):
                                gp.indirect_dma_start(out=kv[:, r, i, :], out_offset=None, in_=kv_tab,
                                                      in_offset=bass.IndirectOffsetOnAxis(
                                                          ap=slot_rec[:, k, BT * b + i, 0:1].bitcast(U32), axis=0),
                                                      bounds_check=N - 1, oob_is_err=False).then_inc(kv_in[r], 16)
                    if has(s, ADD_LAG):
                        d = s - ADD_LAG
                        gp.wait_ge(summed_copied, d + 1)
                        gp.sem_inc(pass_pool, 1)
                        if has(d, 1):
                            gp.wait_ge(added, 16 * d)
                            gp.sem_inc(pass_pool, 1)
                        gp.indirect_dma_start(out=sums, out_offset=bass.IndirectOffsetOnAxis(
                                                  ap=row_i[:, (k - ADD_LAG) % 4, :].bitcast(U32), axis=0),
                                              in_=summed[:, (k - ADD_LAG) % 2, :], in_offset=None, bounds_check=TROWS - 1,
                                              oob_is_err=True, compute_op=ALU.add).then_inc(added, 16)

                gp.wait_ge(kv_clear, 1)
                gp.sem_inc(pass_pool, 1)
                for s in range(2):
                    body(s, s)
                gp.memset(kv[:, 4:, :, :].rearrange("p a b c -> p (a b c)"), 0.0).then_inc(late_clear, 1)
                gp.wait_ge(late_clear, 1)
                gp.sem_inc(pass_pool, 1)
                for s in range(2, PEEL):
                    body(s, s % 4)
                with gp.Fori(*LOOPS) as i:
                    for k in range(4):
                        body(4 * i + k, k)
                for s in range(TAIL_S, NS + ADD_LAG):
                    body(s, s % 4)
                gp.wait_ge(added, 16 * NS)

            @block.scalar
            def _(act):
                def pick(s, b):
                    n = 2 * s + b
                    act.wait_ge(scored, n + 2)
                    if not isinstance(n, int) or n >= 1:
                        act.wait_ge(gathered, n)
                    for block in range(BPT):
                        to, at_ps = (a[:, 1 - b, 0:2 * HD].rearrange("p (m b o) -> p m b o", b=BPT, o=SLOTS)[:, :, block, :]
                                     for a in (own_sc, ps))
                        last = act.activation(to, at_ps, ACT.Copy, scale=take[:, block:block + 1])
                    last.then_inc(picked_act, 1)

                def exp(n, b):
                    act.wait_ge(shifted, n + 1)
                    if not isinstance(n, int) or n >= 2:
                        act.wait_ge(weighed, 2 * n - 2)
                    act.activation(ex[:, b, :, :].rearrange("p g c -> p (g c)"),
                                   se[:, b, :, :].rearrange("p g c -> p (g c)"), ACT.Exp, scale=SCALE).then_inc(exped, 1)

                def spread_at(n, b):
                    if not isinstance(n, int) or n >= 2:
                        act.wait_ge(valued, n - 1)
                    for half in range(2):
                        act.wait_ge(weighed, 2 * n + half + 1)
                        t = slice(2 * half, 2 * half + 2)
                        for q in range(4):
                            r = slice(32 * q, 32 * q + 32)
                            last = act.activation(ad[r, b, 2 * H * half:2 * H * (half + 1), q, :],
                                                  at[r, b, t, :, :].rearrange("p i g c -> p (i g) c"), ACT.Copy)
                        last.then_inc(spread, 1)

                act.wait_ge(kv_clear, 2)

                def body(s, k):
                    par = k % 2
                    if has(s, 0):
                        pick(s, 0)
                    if has(s, 1):
                        spread_at(2 * s - 2, 0)
                    if has(s, 0):
                        exp(2 * s, 0)
                    if has(s, -1):
                        pick(s, 1)
                    if has(s, -2):
                        act.wait_ge(q_turned, s + 3)
                        if has(s, 0):
                            act.wait_ge(scored, 2 * s + 2)
                        for q in range(4):
                            r = slice(32 * q, 32 * q + 32)
                            last = act.activation(qd[r, par, :, q, :], qt[r, :, :], ACT.Copy)
                        last.then_inc(q_spread, 1)
                    if has(s, 1):
                        spread_at(2 * s - 1, 1)
                    if has(s, 0):
                        exp(2 * s + 1, 1)

                for s in range(-2, PEEL):
                    body(s, s % 4)
                with act.Fori(*LOOPS) as i:
                    for k in range(4):
                        body(4 * i + k, k)
                for s in range(TAIL_S, NS + 1):
                    body(s, s % 4)

            @block.tensor
            def _(pe):
                def scores(s, par, b):
                    n = 2 * s + b
                    if b == 0:
                        pe.wait_ge(q_spread, s + 1)
                    pe.wait_ge(k_turned, n + 1)
                    if not isinstance(n, int) or n >= 2:
                        pe.wait_ge(picked_act, n - 1)
                        pe.wait_ge(picked_dve, n - 1)
                    for i in range(BT):
                        last = pe.matmul(ps[:, b, i * HD:(i + 1) * HD], qd[:, par, BT * b + i, :, :].rearrange("p q c -> p (q c)"),
                                         kt[:, b, i * HD:(i + 1) * HD], start=True, stop=True)
                    last.then_inc(scored, 1)

                def values(s, k, b):
                    n = 2 * s + b
                    if b == 0 and has(s, 2):
                        pe.wait_ge(m_turned, s - 1)
                    for half in range(2):
                        pe.wait_ge(spread, 2 * n + half + 1)
                        pe.sem_inc(pass_pe, 1)
                        for g in range(H):
                            for i in range(2 * half, 2 * half + 2):
                                last = pe.matmul(po[32 * i:32 * i + 32, k % 2, P * b:P * b + P],
                                                 kv[:, 2 * k + b, i, HD + g * DH:HD + (g + 1) * DH],
                                                 ad[:, b, H * i + g, :, :].rearrange("p q c -> p (q c)"),
                                                 start=(g == 0), stop=(g == H - 1), tile_position=(0, 32 * i))
                    last.then_inc(valued, 1)

                def gather(n, b):
                    pe.wait_ge(picked_act, n + 1)
                    pe.wait_ge(picked_dve, n + 1)
                    if not isinstance(n, int) or n >= 1:
                        pe.wait_ge(t_turned, n)
                    for i in range(BT):
                        last = pe.matmul(pt[:, 0:HD], gather_h[:, i, :], own_sc[:, b, i * HD:(i + 1) * HD],
                                         start=(i == 0), stop=(i == BT - 1))
                    last.then_inc(gathered, 1)

                def body(s, k):
                    par = k % 2
                    if has(s, 0):
                        scores(s, par, 0)
                    if has(s, 4):
                        pe.wait_ge(m_turned, s - 3)
                    if has(s, 5):
                        pe.wait_ge(summed_copied, s - 4)
                    if has(s, 2):
                        pe.wait_ge(same_built, s - 1)
                    if has(s, 4):
                        pe.matmul(psum_b, same[:, k, :], mt[:, par, :], start=True, stop=True).then_inc(blocks_summed, 1)
                    if has(s, 1):
                        pe.wait_ge(src_floated, s)
                        pe.matmul(prow, src_f[:, 1 - par, :].to_broadcast([P, P]), perm[:, :], start=True, stop=True)
                        pe.matmul(pcol, perm[:, :], src_f[:, 1 - par, :], start=True, stop=True).then_inc(src_rowed, 1)
                    if has(s, 1):
                        gather(2 * s - 1, 1)
                    if has(s, 2):
                        values(s - 2, (k - 2) % 4, 0)
                    if has(s, 0):
                        scores(s, par, 1)
                    if has(s, 0):
                        gather(2 * s, 0)
                    if has(s, 2):
                        values(s - 2, (k - 2) % 4, 1)

                for s in range(PEEL):
                    body(s, s % 4)
                with pe.Fori(*LOOPS) as i:
                    for k in range(4):
                        body(4 * i + k, k)
                for s in range(TAIL_S, NS + 4):
                    body(s, s % 4)

            @block.vector
            def _(dve):
                chain = [0]

                def tick(ins):
                    chain[0] += 1
                    ins.then_inc(DCH, 1)
                    return chain[0]

                def link(ins):
                    dve.wait_ge(DCH, tick(ins))

                dve.memset(qg[:, :, :], 0.0)
                dve.memset(kv[:, 0:4, :, :].rearrange("p a b c -> p (a b c)"), 0.0).then_inc(kv_clear, 1)
                dve.memset(qd[:, :, :, :, :].rearrange("p a j q c -> p (a j q c)"), 0.0)
                dve.tensor_scalar(group_i[:, 0:1], part_i[:, :], 2, None, ALU.logical_shift_right)
                link(dve.tensor_scalar(group_i[:, 1:2], part_i[:, :], BPT - 1, None, ALU.bitwise_and))
                link(dve.tensor_copy(group_f[:, :], group_i[:, :]))
                dve.tensor_scalar(take[:, :], iota_row[:, 0:BPT], group_f[:, 1:2], None, ALU.is_equal)
                link(dve.memset(gather_h[:, :, :].rearrange("p i c -> p (i c)"), 0.0))
                for i in range(BT):
                    last = dve.tensor_scalar(gather_h[:, i, :].rearrange("p (q i h) -> p q i h", q=4, i=BT)[:, :, i, :],
                                             iota_row[:, 0:4 * H].rearrange("p (q h) -> p q h", q=4), group_f[:, 0:1], None, ALU.is_equal)
                link(last)
                dve.tensor_copy(take_s[:, :, :], take[:, :].unsqueeze(2).to_broadcast([P, BPT, SLOTS]))
                dve.memset(ad[:, :, :, :, :].rearrange("p a j q c -> p (a j q c)"), 0.0).then_inc(kv_clear, 1)
                dve.sem_clear(DCH)
                chain[0] = 0

                def turn_k(s, k, b):
                    r = 2 * k + b
                    n = 2 * s + b
                    dve.wait_ge(kv_in[r], uses(s, k, 4, 64))
                    if not isinstance(n, int) or n >= 2:
                        dve.wait_ge(scored, n - 1)
                    dve.transpose(kt[:, b, :].rearrange("p (i c) -> p i c", i=BT), kv[:, r, :, 0:HD]).then_inc(k_turned, 1)

                def turn_q(s, par):
                    dve.wait_ge(q_in[par], uses(s, par, 2, 16))
                    if has(s, 1):
                        dve.wait_ge(q_spread, s)
                    dve.transpose(qt[:, :, :].rearrange("p j (h b) -> p h j b", h=H),
                                  qg[:, par, :].rearrange("p (h j b) -> p h j b", h=H, j=TPS)).then_inc(q_turned, 1)

                def period(s, k, b):
                    par = k % 2
                    n = 2 * s + b
                    now = has(s, 0)
                    old = has(s, 1) if b == 0 else has(s, 0)
                    new = has(s, 0) if b == 0 else has(s, -1)
                    w_par = par if b == 1 else 1 - par
                    ahead = (k + 1) % 4

                    def attention(i):
                        return dve.tensor_tensor(at[:, 1 - b, i, :, :].rearrange("p g (h b) -> p g h b", h=H),
                                                 ex[:, 1 - b, :, H * i:H * i + H].unsqueeze(3).to_broadcast([P, H, H, BPT]),
                                                 rm[:, i, :, :].unsqueeze(1).to_broadcast([P, H, H, BPT]), ALU.mult)

                    if b == 1 and has(s, -2):
                        turn_q(s + 2, par)
                    if now:
                        dve.wait_ge(gathered, n + 1)
                        dve.transpose(se[:, b, :, :].rearrange("p g c -> p (g c)"), pt[:, 0:HD]).then_inc(t_turned, 1)
                    if new:
                        dve.wait_ge(scored, n + 2)
                        to, at_ps = (a[:, 1 - b, 2 * HD:].rearrange("p (m c) -> p m c", c=BPT * SLOTS) for a in (own_sc, ps))
                        dve.tensor_tensor(to, at_ps, take_s[:, :, :].rearrange("p b o -> p (b o)").unsqueeze(1)
                                          .to_broadcast([P, 2 * H, BPT * SLOTS]), ALU.mult).then_inc(picked_dve, 1)
                    if now:
                        dve.wait_ge(t_turned, n + 1)
                        most = tick(dve.tensor_reduce(mx[:, :], se[:, b, :, :].rearrange("p g c -> p c g"), AX.X, ALU.max))
                    if old:
                        dve.wait_ge(exped, n)
                        summed_up = tick(dve.tensor_reduce(den[:, :], ex[:, 1 - b, :, :].rearrange("p g c -> p c g"), AX.X, ALU.add))
                    if now:
                        dve.wait_ge(DCH, most)
                        dve.tensor_tensor(se[:, b, :, :], se[:, b, :, :], mx[:, :].unsqueeze(1).to_broadcast([P, H, BT * H]),
                                          ALU.subtract).then_inc(shifted, 1)
                    if old:
                        dve.wait_ge(DCH, summed_up)
                        inverted = tick(dve.reciprocal(den[:, :], den[:, :]))
                    if b == 0 and has(s, -1):
                        if has(s, 1):
                            dve.wait_ge(src_rowed, s)
                        dve.tensor_copy(src_f[:, 1 - par, :], blk_src[:, ahead, :]).then_inc(src_floated, 1)
                        valid_set = tick(dve.tensor_scalar(valid[:, :], slot_rec[:, ahead, :, 0], float(N), None, ALU.is_lt))
                    if b == 1 and now:
                        dve.wait_ge(src_rowed, s + 1)
                        if has(s, 4):
                            dve.wait_ge(blocks_summed, s - 3)
                        column = tick(dve.tensor_copy(src_b[:, :], pcol))
                    if old:
                        dve.wait_ge(DCH, inverted)
                        weights = tick(dve.tensor_tensor(rm[:, :, :, :],
                                                         den[:, :].rearrange("p (i h) -> p i h", h=H).unsqueeze(3).to_broadcast([P, BT, H, BPT]),
                                                         mask[:, w_par, BT * (1 - b):BT * (1 - b) + BT, :].unsqueeze(2)
                                                         .to_broadcast([P, BT, H, BPT]), ALU.mult))
                    if b == 0 and has(s, -1):
                        turn_k(s + 1, ahead, 1)
                    if b == 1 and has(s, -2):
                        turn_k(s + 2, (k + 2) % 4, 0)
                    if b == 1 and now:
                        dve.wait_ge(DCH, column)
                        dve.tensor_scalar(same[:, k, :], prow, src_b[:, :], None, ALU.is_equal)
                        dve.tensor_scalar(keep[:, 1:2], src_b[:, :], float(N), None, ALU.is_lt)
                        dve.tensor_tensor(row_f[:, :], src_b[:, :], trash[:, :], ALU.subtract)
                        earlier = tick(dve.scalar_tensor_tensor(junk3[:, :], prow, src_b[:, :], below[:, :], ALU.is_equal,
                                                                ALU.mult, accum_out=early_n[:, :]))
                    if old:
                        dve.wait_ge(DCH, weights)
                        if not isinstance(n, int) or n >= 3:
                            dve.wait_ge(spread, 2 * n - 4)
                        attention(0)
                    if b == 0 and has(s, -1):
                        dve.wait_ge(DCH, valid_set)
                        tick(dve.tensor_tensor(mask[:, 1 - par, :, :], valid[:, :].unsqueeze(2).to_broadcast([P, TPS, BPT]),
                                               own[:, :].unsqueeze(1).to_broadcast([P, TPS, BPT]), ALU.mult))
                    if b == 1 and now:
                        dve.wait_ge(DCH, earlier)
                        kept = tick(dve.scalar_tensor_tensor(keep[:, 0:1], early_n[:, :], 0.0, keep[:, 1:2], ALU.is_equal, ALU.mult))
                    if old:
                        attention(1).then_inc(weighed, 1)
                    if b == 1 and now:
                        dve.wait_ge(DCH, kept)
                        row = tick(dve.scalar_tensor_tensor(row_f[:, :], row_f[:, :], keep[:, 0:1], trash[:, :], ALU.mult, ALU.add))
                    if old:
                        attention(2)
                        attention(3).then_inc(weighed, 1)
                    if b == 1 and now:
                        dve.wait_ge(DCH, row)
                        if has(s, 4):
                            dve.wait_ge(added, 16 * (s - 3))
                        dve.tensor_copy(row_i[:, k, :], row_f[:, :]).then_inc(same_built, 1)
                    if b == 0 and has(s, 2):
                        dve.wait_ge(valued, 2 * s - 2)
                        if has(s, 4):
                            dve.wait_ge(blocks_summed, s - 3)
                        dve.transpose(mt[:, par, :], po[:, par, 0:HD].rearrange("p (r h b) -> p h r b", r=TPS, h=H))\
                           .then_inc(m_turned, 1)
                    if b == 1 and has(s, 3):
                        dve.wait_ge(blocks_summed, s - 2)
                        if has(s, 5):
                            dve.wait_ge(added, 16 * (s - 4))
                        dve.tensor_copy(summed[:, 1 - par, :], psum_b).then_inc(summed_copied, 1)

                def body(s, k):
                    period(s, k, 0)
                    period(s, k, 1)
                    if chain[0]:
                        dve.wait_ge(DCH, chain[0])
                        dve.sem_clear(DCH)
                        chain[0] = 0

                for s in range(-2, PEEL):
                    body(s, s % 4)
                with dve.Fori(*LOOPS) as i:
                    for k in range(4):
                        body(4 * i + k, k)
                for s in range(TAIL_S, NS + 3):
                    body(s, s % 4)

        with ExitStack() as c4:
            RING = 4
            xs = sb("xs", [P, NT, D], FP32, c4)
            sq = kv[:, :, :, :].rearrange("p a b c -> p (a b c)")[:, 0:NT * D].rearrange("p (t d) -> p t d", d=D)
            ms = sb("ms", [P, RING, HD], FP32, c4)
            mst = sb("mst", [P, 2, HD], FP32, c4)
            stat = sb("stat", [P, 3, NT], FP32, c4)
            pt4 = c4.enter_context(nc.psum_tensor("pt4", [P, 2, 512], FP32))
            py4 = c4.enter_context(nc.psum_tensor("py4", [P, 2, 512], FP32))
            steps, squared, rooted, y_out = sem("steps"), sem("squared"), sem("rooted"), sem("y_out")
            centred, cleared, varied = sem("centred"), sem("cleared"), sem("varied")
            ms_in = [sem(f"ms_in{i}") for i in range(RING)]
            ms_turned, mst_copied, out_done, x_added = sem("ms_turned"), sem("mst_copied"), sem("out_done"), sem("x_added")
            CHUNKS = 4
            edge = [c * NT // CHUNKS for c in range(CHUNKS + 1)]
            xs_in = [sem(f"xs_in{c}") for c in range(CHUNKS)]
            block = c4.enter_context(nc.Block())

            def after(t, lag):
                return [c for c in range(CHUNKS) if min(edge[c + 1] + lag, NT - 1) == t]

            @block.sync
            def _(sp):
                def load(t, r):
                    sp.dma_start(ms[:, r, :], sums[bass.ds(t * P, P), :]).then_inc(ms_in[r], 16)

                def rows(a, c, hi):
                    return a[edge[c] * P:hi * P, :].rearrange("(t p) d -> p t d", p=P)

                for r in range(RING):
                    load(r, r)
                for c in range(CHUNKS):
                    hi = min(edge[c + 1], NT - 1)
                    sp.dma_start(xs[:, edge[c]:hi, :], rows(x, c, hi)).then_inc(xs_in[c], 16)
                sp.wait_ge(cleared, 1)
                sp.dma_start(xs[0:TAIL, NT - 1, :], x[(NT - 1) * P:N, :]).then_inc(xs_in[CHUNKS - 1], 16)
                with sp.Fori(1, NT // RING) as i:
                    for r in range(RING):
                        sp.wait_ge(ms_turned, RING * i + r - 3)
                        sp.sem_inc(pass_sp, 1)
                        load(RING * i + r, r)
                sp.wait_ge(ms_turned, NT - RING)
                load(NT - 1, 0)
                for c in range(CHUNKS):
                    hi = min(edge[c + 1], NT - 1)
                    sp.wait_ge(steps, c + 1)
                    sp.dma_start(rows(out, c, hi), xs[:, edge[c]:hi, :]).then_inc(y_out, 16)
                sp.dma_start(out[(NT - 1) * P:N, :], xs[0:TAIL, NT - 1, :]).then_inc(y_out, 16)
                sp.wait_ge(y_out, 16 * (CHUNKS + 1))

            @block.tensor
            def _(pe):
                def turn(t, r, uses_r, first):
                    k = r % 2
                    pe.wait_ge(ms_in[r], 16 * uses_r)
                    if not first:
                        pe.wait_ge(mst_copied, t - 1)
                    for c in range(2):
                        last = pe.transpose(pt4[:, k, c * P:(c + 1) * P], ms[:, r, c * P:(c + 1) * P], ident[:, :])
                    last.then_inc(ms_turned, 1)

                def project(t, k, first):
                    pe.wait_ge(mst_copied, t + 1)
                    if not first:
                        pe.wait_ge(x_added, t - 1)
                    for c in range(2):
                        last = pe.matmul(py4[:, k, 0:D], mst[:, k, c * P:(c + 1) * P], wot[:, c, :], start=(c == 0), stop=(c == 1))
                    last.then_inc(out_done, 1)

                turn(0, 0, 1, True)
                for t in range(RING):
                    turn(t + 1, (t + 1) % RING, (t + 1) // RING + 1, t < 1)
                    project(t, t % 2, t < 2)
                with pe.Fori(1, NT // RING) as i:
                    for r in range(RING):
                        turn(RING * i + r + 1, (r + 1) % RING, i + 1 + (r + 1) // RING, False)
                        project(RING * i + r, r % 2, False)
                project(NT - 1, 0, False)

            @block.scalar
            def _(act):
                for t in range(NT):
                    act.wait_ge(ms_turned, t + 1)
                    if t >= 2:
                        act.wait_ge(out_done, t - 1)
                    act.activation(mst[:, t % 2, :], pt4[:, t % 2, 0:HD], ACT.Copy).then_inc(mst_copied, 1)
                    for c in range(CHUNKS):
                        tiles = slice(edge[c], edge[c + 1])
                        if c in after(t, 4):
                            act.wait_ge(centred, c + 1)
                            act.activation(sq[:, tiles, :], xs[:, tiles, :], ACT.Square).then_inc(squared, 1)
                        if c in after(t, 8):
                            act.wait_ge(varied, c + 1)
                            act.activation(stat[:, 1, tiles], stat[:, 0, tiles], ACT.Sqrt).then_inc(rooted, 1)

            @block.vector
            def _(dve):
                chain = [0]

                def tick(ins):
                    chain[0] += 1
                    ins.then_inc(DCH, 1)
                    return chain[0]

                def link(ins):
                    dve.wait_ge(DCH, tick(ins))

                def per_row(c):
                    return stat[:, 2, edge[c]:edge[c + 1]].unsqueeze(2).to_broadcast([P, edge[c + 1] - edge[c], D])

                dve.memset(xs[:, NT - 1, :], 0.0).then_inc(cleared, 1)
                kind_added = {}
                for u in range(NT + KINDS):
                    for k in range(KINDS):
                        t = u - k
                        if 0 <= t < NT:
                            if k:
                                dve.wait_ge(DCH, kind_added[t])
                            elif t in edge:
                                c = edge.index(t)
                                dve.wait_ge(xs_in[c], 32 if c == CHUNKS - 1 else 16)
                            kind_added[t] = tick(dve.scalar_tensor_tensor(xs[:, t, :], kindw[:, k, :], counts[:, k, t:t + 1],
                                                                          xs[:, t, :], ALU.mult, ALU.add))
                    t = u - KINDS
                    if t < 0:
                        continue
                    dve.wait_ge(DCH, kind_added[t])
                    dve.wait_ge(out_done, t + 1)
                    dve.tensor_tensor(xs[:, t, :], py4[:, t % 2, 0:D], xs[:, t, :], ALU.add).then_inc(x_added, 1)
                    for c in range(CHUNKS):
                        tiles = slice(edge[c], edge[c + 1])
                        if t == edge[c + 1] - 1:
                            dve.wait_ge(x_added, t + 1)
                            link(dve.tensor_reduce(stat[:, 2, tiles], xs[:, tiles, :], AX.X, ALU.add))
                            link(dve.tensor_scalar(stat[:, 2, tiles], stat[:, 2, tiles], 1.0 / D, None, ALU.mult))
                            dve.tensor_tensor(xs[:, tiles, :], xs[:, tiles, :], per_row(c), ALU.subtract).then_inc(centred, 1)
                        if c in after(t, 6):
                            dve.wait_ge(squared, c + 1)
                            link(dve.tensor_reduce(stat[:, 2, tiles], sq[:, tiles, :], AX.X, ALU.add))
                            dve.tensor_scalar(stat[:, 0, tiles], stat[:, 2, tiles], 1.0 / D, EPS, ALU.mult, ALU.add).then_inc(varied, 1)
                        if c in after(t, 9):
                            dve.wait_ge(rooted, c + 1)
                            link(dve.reciprocal(stat[:, 2, tiles], stat[:, 1, tiles]))
                            dve.tensor_tensor(xs[:, tiles, :], xs[:, tiles, :], per_row(c), ALU.mult).then_inc(steps, 1)


_INS = ["x", "src", "dst", "edge_type_3", "L0_gnn_Wq", "L0_gnn_bq", "L0_gnn_Wk", "L0_gnn_bk", "L0_gnn_Wv", "L0_gnn_bv",
        "L0_gnn_edge_emb", "L0_gnn_Wo", "L0_gnn_bo"]


def kernel(**inputs):
    import numpy as _np
    import concourse.bacc as _bacc
    from concourse import mybir as _mybir
    from concourse.bass_utils import run_bass_kernel_spmd as _run

    nc = _bacc.Bacc("TRN2", target_bir_lowering=False, num_devices=1)
    arrays, args = {}, []
    for name in _INS:
        a = _np.ascontiguousarray(inputs[name])
        arrays[f"in_{name}_dram"] = a
        args.append(nc.dram_tensor(f"in_{name}_dram", a.shape, _mybir.dt.from_np(a.dtype), kind="ExternalInput").ap())
    args.append(nc.dram_tensor("out_0_dram", (N, D), _mybir.dt.float32, kind="ExternalOutput").ap())
    build(nc, *args)
    r = _run(nc, [arrays], core_ids=[0])
    return r.results[0]["out_0_dram"]
```
